# Optimizing a Trainium2 kernel written in Bass

```python
import numpy as np
import jax
import jax.numpy as jnp

def _softmax(x, axis=-1):
    return jax.nn.softmax(x, axis=axis)
def _gelu(x):
    return jax.nn.gelu(x, approximate=True)
def _silu(x):
    return jax.nn.silu(x)
def _sigmoid(x):
    return jax.nn.sigmoid(x)
def _layernorm(x, axis=-1, eps=1e-5):
    m = jnp.mean(x, axis=axis, keepdims=True)
    v = jnp.var(x, axis=axis, keepdims=True)
    return (x - m) / jnp.sqrt(v + eps)
def _scatter_add(tgt, idx, src, axis=0):
    return tgt.at[idx].add(src)
def _segment_sum(src, seg, n):
    return jax.ops.segment_sum(src, seg, n)

kernel_name = 'mk_conv_attn_hybrid_d4_conv_nhwc128_c0e06e'

def setup_inputs(seed: int = 0):
    np.random.seed(seed)
    _w = jnp.asarray
    def _rec_inputs():
        import jax
        import jax.numpy as jnp
        _gk = jax.random.key(seed)
        x = -0.0005207 + 1.001 * jax.random.normal(jax.random.fold_in(_gk, 1), (4, 64, 64, 128), jnp.float32)
        return x
    x = _rec_inputs()
    def _L0_conv_setup():
        import jax, jax.numpy as jnp
        import numpy as np
        B, H, W, C = (4, 64, 64, 128)
        G = 4
        HC = C // G
        K = 3
        K2 = K * K
        PAD = K // 2
        SCALE = HC ** (-0.5)

        def conv2d(x, w, padding=1, dilation=1, groups=1):
            return jax.lax.conv_general_dilated(x, w, (1, 1), [(padding, padding), (padding, padding)], rhs_dilation=(dilation, dilation), dimension_numbers=('NCHW', 'OIHW', 'NCHW'), feature_group_count=groups)

        def pconv(x, w):
            c4 = w.shape[0]
            return jnp.concatenate([conv2d(x[:, :c4], w, padding=1), x[:, c4:]], axis=1)

        def conv1x1(x, w, b):
            return jnp.einsum('bchw,oc->bohw', x, w) + b[None, :, None, None]

        def deform_sample(img, offset, mask, dilation, pad):
            b, cg, h, w = img.shape
            ky, kx = jnp.meshgrid(jnp.arange(K), jnp.arange(K), indexing='ij')
            base_y = (ky.reshape(-1) * dilation - pad).astype(img.dtype)
            base_x = (kx.reshape(-1) * dilation - pad).astype(img.dtype)
            off = offset.reshape(b, K2, 2, h, w)
            py = jnp.arange(h, dtype=img.dtype)[None, None, :, None] + base_y[None, :, None, None] + off[:, :, 0]
            px = jnp.arange(w, dtype=img.dtype)[None, None, None, :] + base_x[None, :, None, None] + off[:, :, 1]
            y0 = jnp.floor(py)
            x0 = jnp.floor(px)
            wy = py - y0
            wx = px - x0
            flat = img.reshape(b, cg, h * w)

            def gather(iy, ix):
                valid = ((iy >= 0) & (iy < h) & (ix >= 0) & (ix < w)).astype(img.dtype)
                idx = (jnp.clip(iy, 0, h - 1) * w + jnp.clip(ix, 0, w - 1)).astype(jnp.int32)
                g = jax.vmap(lambda f, i: jnp.take(f, i, axis=1))(flat, idx.reshape(b, -1))
                return g.reshape(b, cg, K2, h, w) * valid[:, None]
            wy_ = wy[:, None]
            wx_ = wx[:, None]
            out = gather(y0, x0) * (1 - wy_) * (1 - wx_) + gather(y0, x0 + 1) * (1 - wy_) * wx_ + gather(y0 + 1, x0) * wy_ * (1 - wx_) + gather(y0 + 1, x0 + 1) * wy_ * wx_
            return out * mask[:, None]
        key = jax.random.key(seed)
        ks = jax.random.split(key, 14)
        d = {}
        d['x'] = jax.random.normal(ks[0], (B, H, W, C), jnp.float32)
        d['w_qkv'] = jax.random.normal(ks[1], (C, 3 * C), jnp.float32) * C ** (-0.5)
        d['b_qkv'] = jax.random.normal(ks[2], (3 * C,), jnp.float32) * 0.02
        d['w_dw'] = jax.random.normal(ks[3], (3 * C, 1, 3, 3), jnp.float32) * 0.2
        d['b_dw'] = jax.random.normal(ks[4], (3 * C,), jnp.float32) * 0.02
        d['pconv_off_w'] = jax.random.normal(ks[5], (G, C // 4, C // 4, 3, 3), jnp.float32) * 0.05
        d['w_off'] = jax.random.normal(ks[6], (G, 2 * K2, C), jnp.float32) * 0.01
        d['b_off'] = jax.random.normal(ks[7], (G, 2 * K2), jnp.float32) * 0.01
        d['pconv_mask_w'] = jax.random.normal(ks[8], (C // 4, C // 4, 3, 3), jnp.float32) * 0.05
        d['w_mask'] = jax.random.normal(ks[9], (K2, C), jnp.float32) * 0.01
        d['b_mask'] = jax.random.normal(ks[10], (K2,), jnp.float32) * 0.01
        d['w_proj'] = jax.random.normal(ks[11], (C, C), jnp.float32) * C ** (-0.5)
        d['b_proj'] = jax.random.normal(ks[12], (C,), jnp.float32) * 0.02
        return d
    _L0_conv_all = _L0_conv_setup()
    _L0_conv_in = {k: v for k, v in _L0_conv_all.items() if k in ('w_qkv', 'b_qkv', 'w_dw', 'b_dw', 'pconv_off_w', 'w_off', 'b_off', 'pconv_mask_w', 'w_mask', 'b_mask', 'w_proj', 'b_proj', )}
    del _L0_conv_all

    def _L1_conv_setup():
        import jax, jax.numpy as jnp
        import numpy as np
        HEADS = 4
        DIM_HEAD = 32
        DIM = HEADS * DIM_HEAD
        B, H, W, C = (32, 64, 64, 128)
        LN_EPS = 1e-05
        key = jax.random.key(seed)
        k0, k1, k2, k3, k4 = jax.random.split(key, 5)
        x = jax.random.normal(k0, (B, H, W, C), dtype=jnp.float32)
        w_qkv = jax.random.normal(k1, (C, DIM * 3), dtype=jnp.float32) * (1.0 / np.sqrt(C))
        w_out = jax.random.normal(k2, (DIM, C), dtype=jnp.float32) * (1.0 / np.sqrt(DIM))
        b_out = jax.random.normal(k3, (C,), dtype=jnp.float32) * 0.01
        ln_scale = jnp.ones((C,), dtype=jnp.float32)
        return {'x': x, 'w_qkv': w_qkv, 'w_out': w_out, 'b_out': b_out, 'ln_scale': ln_scale}
    _L1_conv_all = _L1_conv_setup()
    _L1_conv_in = {k: v for k, v in _L1_conv_all.items() if k in ('w_qkv', 'w_out', 'b_out', 'ln_scale', )}
    del _L1_conv_all

    def _L2_attn_setup():
        import jax, jax.numpy as jnp
        import numpy as np
        B, N, D = (4, 1024, 128)
        key = jax.random.key(seed)
        ks = jax.random.split(key, 4)
        scale = 1.0 / np.sqrt(D)
        return {'inputs': jax.random.normal(ks[0], (B, N, D), dtype=jnp.float32), 'Wq': jax.random.normal(ks[1], (D, D), dtype=jnp.float32) * scale, 'bq': jnp.zeros((D,), dtype=jnp.float32), 'Wk': jax.random.normal(ks[2], (D, D), dtype=jnp.float32) * scale, 'bk': jnp.zeros((D,), dtype=jnp.float32), 'Wv': jax.random.normal(ks[3], (D, D), dtype=jnp.float32) * scale, 'bv': jnp.zeros((D,), dtype=jnp.float32)}
    _L2_attn_all = _L2_attn_setup()
    _L2_attn_in = {k: v for k, v in _L2_attn_all.items() if k in ('Wq', 'bq', 'Wk', 'bk', 'Wv', 'bv', )}
    del _L2_attn_all

    def _L2_ffn_setup():
        import jax, jax.numpy as jnp
        import numpy as np
        B, S, D, E, H, O, K = (512, 2048, 128, 64, 512, 128, 8)
        key = jax.random.key(seed)
        k0, k1, k2, k3 = jax.random.split(key, 4)
        x = jax.random.normal(k0, (B, S, D), dtype=jnp.float32)
        gate_w = jax.random.normal(k1, (E, D), dtype=jnp.float32) * (1.0 / np.sqrt(D))
        gate_b = jnp.zeros((E,), dtype=jnp.float32)
        weight1 = jax.random.uniform(k2, (E, D + 1, H), dtype=jnp.float32, minval=-1.0, maxval=1.0) * (1.0 / np.sqrt(D + 1))
        weight2 = jax.random.uniform(k3, (E, H + 1, O), dtype=jnp.float32, minval=-1.0, maxval=1.0) * (1.0 / np.sqrt(H + 1))
        return {'x': x, 'gate_w': gate_w, 'gate_b': gate_b, 'weight1': weight1, 'weight2': weight2}
    _L2_ffn_all = _L2_ffn_setup()
    _L2_ffn_in = {k: v for k, v in _L2_ffn_all.items() if k in ('gate_w', 'gate_b', 'weight1', 'weight2', )}
    del _L2_ffn_all

    def _L3_attn_setup():
        import jax, jax.numpy as jnp
        import numpy as np
        B, T, D = (4, 2048, 128)
        key = jax.random.key(seed)
        k1, k2, k3 = jax.random.split(key, 3)
        x = jax.random.normal(k1, (B, T, D), dtype=jnp.float32)
        lim = 1.0 / np.sqrt(D)
        W = jax.random.uniform(k2, (3 * D, D), dtype=jnp.float32, minval=-lim, maxval=lim)
        b = jax.random.uniform(k3, (3 * D,), dtype=jnp.float32, minval=-lim, maxval=lim)
        return {'x': x, 'W': W, 'b': b}
    _L3_attn_all = _L3_attn_setup()
    _L3_attn_in = {k: v for k, v in _L3_attn_all.items() if k in ('W', 'b', )}
    del _L3_attn_all

    def _L3_ffn_setup():
        import jax, jax.numpy as jnp
        import numpy as np
        PADDED_SL = 8192
        TEMPERATURE = 1.0
        SIGMA_POW = 0.25

        def _stu_conv(phi, u, n):
            b, sl, d = u.shape
            sgn = jnp.where(jnp.arange(sl) % 2 == 0, 1.0, -1.0).astype(u.dtype)
            sgn3 = sgn[None, :, None]
            Vf = jnp.fft.rfft(phi, n=n, axis=0)
            Uf_p = jnp.fft.rfft(u, n=n, axis=1)
            Uf_m = jnp.fft.rfft(u * sgn3, n=n, axis=1)
            U_plus = jnp.fft.irfft(Vf[None, :, :, None] * Uf_p[:, :, None, :], n=n, axis=1)[:, :sl]
            U_minus = jnp.fft.irfft(Vf[None, :, :, None] * Uf_m[:, :, None, :], n=n, axis=1)[:, :sl]
            U_minus = U_minus * sgn[None, :, None, None]
            return (U_plus, U_minus)

        def _compute_spectral(u, sigma, phi, Mpp, Mpm):
            U_plus, U_minus = _stu_conv(phi, u, PADDED_SL)
            s = sigma ** SIGMA_POW
            out = jnp.einsum('btkd,k,kde->bte', U_plus, s, Mpp)
            out = out + jnp.einsum('btkd,k,kde->bte', U_minus, s, Mpm)
            return out

        def _compute_ar_u(Mu, u):
            sl = u.shape[1]
            out = jnp.zeros(u.shape[:2] + (Mu.shape[-1],), dtype=u.dtype)
            for i in range(Mu.shape[0]):
                ui = jnp.pad(u, ((0, 0), (i, 0), (0, 0)))[:, :sl]
                out = out + jnp.einsum('btd,de->bte', ui, Mu[i])
            return out

        def _stu(u, sigma, phi, Mu, Mpp, Mpm):
            return _compute_spectral(u, sigma, phi, Mpp, Mpm) + _compute_ar_u(Mu, u)
        key = jax.random.key(seed)
        ks = jax.random.split(key, 8)
        b, sl, d, K, k_u = (2, 4096, 128, 16, 3)
        x = jax.random.normal(ks[0], (b, sl, d), dtype=jnp.float32)
        sigma = jax.random.uniform(ks[1], (K,), dtype=jnp.float32, minval=0.001, maxval=1.0)
        phi = jax.random.normal(ks[2], (sl, K), dtype=jnp.float32) / np.sqrt(sl)
        M_u = jax.random.normal(ks[3], (4, k_u, d, d), dtype=jnp.float32) * 0.02
        M_phi_plus = jax.random.normal(ks[4], (4, K, d, d), dtype=jnp.float32) * 0.02
        M_phi_minus = jax.random.normal(ks[5], (4, K, d, d), dtype=jnp.float32) * 0.02
        log_weights = jnp.ones((4,), dtype=jnp.float32)
        u01 = jax.random.uniform(ks[6], (4,), dtype=jnp.float32, minval=1e-06, maxval=1.0 - 1e-06)
        gumbel = -jnp.log(-jnp.log(u01))
        return {'x': x, 'sigma': sigma, 'phi': phi, 'M_u': M_u, 'M_phi_plus': M_phi_plus, 'M_phi_minus': M_phi_minus, 'log_weights': log_weights, 'gumbel': gumbel}
    _L3_ffn_all = _L3_ffn_setup()
    _L3_ffn_in = {k: v for k, v in _L3_ffn_all.items() if k in ('sigma', 'phi', 'M_u', 'M_phi_plus', 'M_phi_minus', 'log_weights', 'gumbel', )}
    del _L3_ffn_all

    return {
        "x": x,
        "L0_conv_w_qkv": _L0_conv_in["w_qkv"],
        "L0_conv_b_qkv": _L0_conv_in["b_qkv"],
        "L0_conv_w_dw": _L0_conv_in["w_dw"],
        "L0_conv_b_dw": _L0_conv_in["b_dw"],
        "L0_conv_pconv_off_w": _L0_conv_in["pconv_off_w"],
        "L0_conv_w_off": _L0_conv_in["w_off"],
        "L0_conv_b_off": _L0_conv_in["b_off"],
        "L0_conv_pconv_mask_w": _L0_conv_in["pconv_mask_w"],
        "L0_conv_w_mask": _L0_conv_in["w_mask"],
        "L0_conv_b_mask": _L0_conv_in["b_mask"],
        "L0_conv_w_proj": _L0_conv_in["w_proj"],
        "L0_conv_b_proj": _L0_conv_in["b_proj"],
        "L1_conv_w_qkv": _L1_conv_in["w_qkv"],
        "L1_conv_w_out": _L1_conv_in["w_out"],
        "L1_conv_b_out": _L1_conv_in["b_out"],
        "L1_conv_ln_scale": _L1_conv_in["ln_scale"],
        "L2_attn_Wq": _L2_attn_in["Wq"],
        "L2_attn_bq": _L2_attn_in["bq"],
        "L2_attn_Wk": _L2_attn_in["Wk"],
        "L2_attn_bk": _L2_attn_in["bk"],
        "L2_attn_Wv": _L2_attn_in["Wv"],
        "L2_attn_bv": _L2_attn_in["bv"],
        "L2_ffn_gate_w": _L2_ffn_in["gate_w"],
        "L2_ffn_gate_b": _L2_ffn_in["gate_b"],
        "L2_ffn_weight1": _L2_ffn_in["weight1"],
        "L2_ffn_weight2": _L2_ffn_in["weight2"],
        "L3_attn_W": _L3_attn_in["W"],
        "L3_attn_b": _L3_attn_in["b"],
        "L3_ffn_sigma": _L3_ffn_in["sigma"],
        "L3_ffn_phi": _L3_ffn_in["phi"],
        "L3_ffn_M_u": _L3_ffn_in["M_u"],
        "L3_ffn_M_phi_plus": _L3_ffn_in["M_phi_plus"],
        "L3_ffn_M_phi_minus": _L3_ffn_in["M_phi_minus"],
        "L3_ffn_log_weights": _L3_ffn_in["log_weights"],
        "L3_ffn_gumbel": _L3_ffn_in["gumbel"],
    }

def reference(x, L0_conv_w_qkv, L0_conv_b_qkv, L0_conv_w_dw, L0_conv_b_dw, L0_conv_pconv_off_w, L0_conv_w_off, L0_conv_b_off, L0_conv_pconv_mask_w, L0_conv_w_mask, L0_conv_b_mask, L0_conv_w_proj, L0_conv_b_proj, L1_conv_w_qkv, L1_conv_w_out, L1_conv_b_out, L1_conv_ln_scale, L2_attn_Wq, L2_attn_bq, L2_attn_Wk, L2_attn_bk, L2_attn_Wv, L2_attn_bv, L2_ffn_gate_w, L2_ffn_gate_b, L2_ffn_weight1, L2_ffn_weight2, L3_attn_W, L3_attn_b, L3_ffn_sigma, L3_ffn_phi, L3_ffn_M_u, L3_ffn_M_phi_plus, L3_ffn_M_phi_minus, L3_ffn_log_weights, L3_ffn_gumbel):
    import jax
    import jax.numpy as jnp
    def _L0_conv_ref(x, w_qkv, b_qkv, w_dw, b_dw, pconv_off_w, w_off, b_off, pconv_mask_w, w_mask, b_mask, w_proj, b_proj):
        import jax, jax.numpy as jnp
        import numpy as np
        B, H, W, C = (4, 64, 64, 128)
        G = 4
        HC = C // G
        K = 3
        K2 = K * K
        PAD = K // 2
        SCALE = HC ** (-0.5)

        def conv2d(x, w, padding=1, dilation=1, groups=1):
            return jax.lax.conv_general_dilated(x, w, (1, 1), [(padding, padding), (padding, padding)], rhs_dilation=(dilation, dilation), dimension_numbers=('NCHW', 'OIHW', 'NCHW'), feature_group_count=groups)

        def pconv(x, w):
            c4 = w.shape[0]
            return jnp.concatenate([conv2d(x[:, :c4], w, padding=1), x[:, c4:]], axis=1)

        def conv1x1(x, w, b):
            return jnp.einsum('bchw,oc->bohw', x, w) + b[None, :, None, None]

        def deform_sample(img, offset, mask, dilation, pad):
            b, cg, h, w = img.shape
            ky, kx = jnp.meshgrid(jnp.arange(K), jnp.arange(K), indexing='ij')
            base_y = (ky.reshape(-1) * dilation - pad).astype(img.dtype)
            base_x = (kx.reshape(-1) * dilation - pad).astype(img.dtype)
            off = offset.reshape(b, K2, 2, h, w)
            py = jnp.arange(h, dtype=img.dtype)[None, None, :, None] + base_y[None, :, None, None] + off[:, :, 0]
            px = jnp.arange(w, dtype=img.dtype)[None, None, None, :] + base_x[None, :, None, None] + off[:, :, 1]
            y0 = jnp.floor(py)
            x0 = jnp.floor(px)
            wy = py - y0
            wx = px - x0
            flat = img.reshape(b, cg, h * w)

            def gather(iy, ix):
                valid = ((iy >= 0) & (iy < h) & (ix >= 0) & (ix < w)).astype(img.dtype)
                idx = (jnp.clip(iy, 0, h - 1) * w + jnp.clip(ix, 0, w - 1)).astype(jnp.int32)
                g = jax.vmap(lambda f, i: jnp.take(f, i, axis=1))(flat, idx.reshape(b, -1))
                return g.reshape(b, cg, K2, h, w) * valid[:, None]
            wy_ = wy[:, None]
            wx_ = wx[:, None]
            out = gather(y0, x0) * (1 - wy_) * (1 - wx_) + gather(y0, x0 + 1) * (1 - wy_) * wx_ + gather(y0 + 1, x0) * wy_ * (1 - wx_) + gather(y0 + 1, x0 + 1) * wy_ * wx_
            return out * mask[:, None]
        b, h, w, c = x.shape
        n = h * w
        qkv = x @ w_qkv + b_qkv
        qkv = conv2d(qkv.transpose(0, 3, 1, 2), w_dw, padding=1, groups=3 * c) + b_dw[None, :, None, None]
        qkv = qkv.transpose(0, 2, 3, 1)
        q = qkv[..., :c]
        kv = qkv[..., c:].reshape(b, h, w, 2, G, HC).transpose(3, 0, 4, 5, 1, 2)
        q_img = q.transpose(0, 3, 1, 2)
        mask = jax.nn.sigmoid(conv1x1(pconv(q_img, pconv_mask_w), w_mask, b_mask))
        k_list, v_list = ([], [])
        for i in range(G):
            off = conv1x1(pconv(q_img, pconv_off_w[i]), w_off[i], b_off[i])
            dil = 2 * i + 1
            k_list.append(deform_sample(kv[0, :, i], off, mask, dil, dil * PAD))
            v_list.append(deform_sample(kv[1, :, i], off, mask, dil, dil * PAD))
        ks_ = jnp.stack(k_list, 1).reshape(b, G, HC, K2, n)
        vs_ = jnp.stack(v_list, 1).reshape(b, G, HC, K2, n)
        qf = (q.reshape(b, n, G, HC) * SCALE).transpose(0, 2, 1, 3)
        attn = jax.nn.softmax(jnp.einsum('bgnc,bgckn->bgnk', qf, ks_), axis=-1)
        out = jnp.einsum('bgnk,bgckn->bgnc', attn, vs_)
        out = out.transpose(0, 2, 1, 3).reshape(b, h, w, c)
        return out @ w_proj + b_proj

    def _L1_conv_ref(x, w_qkv, w_out, b_out, ln_scale):
        import jax, jax.numpy as jnp
        import numpy as np
        HEADS = 4
        DIM_HEAD = 32
        DIM = HEADS * DIM_HEAD
        B, H, W, C = (32, 64, 64, 128)
        LN_EPS = 1e-05
        b, h, w, c = x.shape
        n = h * w
        qkv = jnp.einsum('bhwc,cf->bhwf', x, w_qkv)
        q, k, v = jnp.split(qkv, 3, axis=-1)
        q = q.reshape(b, n, HEADS, DIM_HEAD)
        k = k.reshape(b, n, HEADS, DIM_HEAD)
        v = v.reshape(b, n, HEADS, DIM_HEAD)
        q = jax.nn.softmax(q, axis=-1) * (1.0 / np.sqrt(DIM_HEAD))
        k = jax.nn.softmax(k, axis=1)
        v = v * (1.0 / n)
        context = jnp.einsum('bnhd,bnhe->bhde', k, v)
        out = jnp.einsum('bhde,bnhd->bnhe', context, q)
        out = out.reshape(b, h, w, DIM)
        out = jnp.einsum('bhwd,dc->bhwc', out, w_out) + b_out
        mu = jnp.mean(out, axis=-1, keepdims=True)
        var = jnp.mean(jnp.square(out - mu), axis=-1, keepdims=True)
        out = (out - mu) * jax.lax.rsqrt(var + LN_EPS) * ln_scale
        return out

    def _L2_attn_ref(inputs, Wq, bq, Wk, bk, Wv, bv):
        import jax, jax.numpy as jnp
        import numpy as np
        B, N, D = (4, 1024, 128)
        q = inputs @ Wq + bq
        k = inputs @ Wk + bk
        v = inputs @ Wv + bv
        kv = jnp.sum(k * v, axis=1, keepdims=True)
        return q * kv

    def _L2_ffn_ref(x, gate_w, gate_b, weight1, weight2):
        import jax, jax.numpy as jnp
        import numpy as np
        B, S, D, E, H, O, K = (512, 2048, 128, 64, 512, 128, 8)
        Bn, Sn, Dn = x.shape
        logits = jnp.einsum('bsd,ed->bse', x, gate_w) + gate_b
        probs = jax.nn.softmax(logits, axis=1)
        vals, idx = jax.lax.top_k(probs.transpose(0, 2, 1), K)
        topv = vals.transpose(0, 2, 1)
        topi = idx.transpose(0, 2, 1)
        flat_idx = topi.reshape(Bn, K * E)
        gathered = jnp.take_along_axis(x, flat_idx[:, :, None], axis=1)
        gathered = gathered.reshape(Bn, K, E, Dn)
        pooled = jnp.einsum('bked,bke->bed', gathered, topv)
        ones = jnp.ones((E, Bn, 1), dtype=x.dtype)
        h = jnp.concatenate([pooled.transpose(1, 0, 2), ones], axis=-1)
        h = jax.nn.gelu(jnp.einsum('ebd,edh->ebh', h, weight1), approximate=False)
        h = jnp.concatenate([h, ones], axis=-1)
        out = jnp.einsum('ebh,eho->ebo', h, weight2)
        out = out.transpose(1, 0, 2)
        weighted = jnp.einsum('beo,bke->bkeo', out, topv).reshape(Bn, K * E, O)
        outputs = jnp.zeros((Bn, Sn, O), dtype=x.dtype)
        outputs = outputs.at[jnp.arange(Bn)[:, None], flat_idx].add(weighted)
        return outputs

    def _L3_attn_ref(x, W, b):
        import jax, jax.numpy as jnp
        import numpy as np
        B, T, D = (4, 2048, 128)
        Bx, Tx, Dx = x.shape
        qkv = (x @ W.T + b).reshape(Bx, Tx, 3, Dx)
        q, k, v = (qkv[:, :, 0], qkv[:, :, 1], qkv[:, :, 2])
        q = jax.nn.elu(q) + 1.0
        k = jax.nn.elu(k) + 1.0
        kv = jnp.einsum('bti,btj->btij', k, v)
        kv_cum = jnp.cumsum(kv, axis=1)
        k_cum = jnp.cumsum(k, axis=1)
        num = jnp.einsum('bti,btij->btj', q, kv_cum)
        den = jnp.einsum('bti,bti->bt', q, k_cum)[..., None] + 1e-06
        return num / den

    def _L3_ffn_ref(x, sigma, phi, M_u, M_phi_plus, M_phi_minus, log_weights, gumbel):
        import jax, jax.numpy as jnp
        import numpy as np
        PADDED_SL = 8192
        TEMPERATURE = 1.0
        SIGMA_POW = 0.25

        def _stu_conv(phi, u, n):
            b, sl, d = u.shape
            sgn = jnp.where(jnp.arange(sl) % 2 == 0, 1.0, -1.0).astype(u.dtype)
            sgn3 = sgn[None, :, None]
            Vf = jnp.fft.rfft(phi, n=n, axis=0)
            Uf_p = jnp.fft.rfft(u, n=n, axis=1)
            Uf_m = jnp.fft.rfft(u * sgn3, n=n, axis=1)
            U_plus = jnp.fft.irfft(Vf[None, :, :, None] * Uf_p[:, :, None, :], n=n, axis=1)[:, :sl]
            U_minus = jnp.fft.irfft(Vf[None, :, :, None] * Uf_m[:, :, None, :], n=n, axis=1)[:, :sl]
            U_minus = U_minus * sgn[None, :, None, None]
            return (U_plus, U_minus)

        def _compute_spectral(u, sigma, phi, Mpp, Mpm):
            U_plus, U_minus = _stu_conv(phi, u, PADDED_SL)
            s = sigma ** SIGMA_POW
            out = jnp.einsum('btkd,k,kde->bte', U_plus, s, Mpp)
            out = out + jnp.einsum('btkd,k,kde->bte', U_minus, s, Mpm)
            return out

        def _compute_ar_u(Mu, u):
            sl = u.shape[1]
            out = jnp.zeros(u.shape[:2] + (Mu.shape[-1],), dtype=u.dtype)
            for i in range(Mu.shape[0]):
                ui = jnp.pad(u, ((0, 0), (i, 0), (0, 0)))[:, :sl]
                out = out + jnp.einsum('btd,de->bte', ui, Mu[i])
            return out

        def _stu(u, sigma, phi, Mu, Mpp, Mpm):
            return _compute_spectral(u, sigma, phi, Mpp, Mpm) + _compute_ar_u(Mu, u)
        T = x.shape[1]
        outs = []
        for i, frac in enumerate((1, 2, 4, 8)):
            xi = x[:, :T // frac]
            si = _stu(xi, sigma, phi, M_u[i], M_phi_plus[i], M_phi_minus[i])
            si = jnp.pad(si, ((0, 0), (0, T - si.shape[1]), (0, 0)))
            outs.append(si)
        y_soft = jax.nn.softmax((log_weights + gumbel) / TEMPERATURE)
        y_hard = jax.nn.one_hot(jnp.argmax(y_soft), 4, dtype=y_soft.dtype)
        weights = y_hard - jax.lax.stop_gradient(y_soft) + y_soft
        stacked = jnp.stack(outs, axis=-1)
        return jnp.sum(stacked * weights, axis=-1)

    def _gn(v, G=32, eps=1e-5):
        B_, H_, W_, C_ = v.shape
        g = v.reshape(B_, H_, W_, G, C_ // G)
        m = jnp.mean(g, axis=(1, 2, 4), keepdims=True)
        s = jnp.var(g, axis=(1, 2, 4), keepdims=True)
        return ((g - m) / jnp.sqrt(s + eps)).reshape(v.shape)

    def _ln_c(v, eps=1e-6):
        m = jnp.mean(v, axis=-1, keepdims=True)
        s = jnp.var(v, axis=-1, keepdims=True)
        return (v - m) / jnp.sqrt(s + eps)

    def _ln_t(v, eps=1e-5):
        m = jnp.mean(v, axis=-1, keepdims=True)
        s = jnp.var(v, axis=-1, keepdims=True)
        return (v - m) / jnp.sqrt(s + eps)

    def _to_tokens(v):
        B_, H_, W_, C_ = v.shape
        return v.reshape(B_, H_ * W_, C_)
    def _from_tokens(t, like):
        return t.reshape(like.shape)

    x = x + _L0_conv_ref(_gn(x), L0_conv_w_qkv, L0_conv_b_qkv, L0_conv_w_dw, L0_conv_b_dw, L0_conv_pconv_off_w, L0_conv_w_off, L0_conv_b_off, L0_conv_pconv_mask_w, L0_conv_w_mask, L0_conv_b_mask, L0_conv_w_proj, L0_conv_b_proj)
    x = x + _L1_conv_ref(_gn(x), L1_conv_w_qkv, L1_conv_w_out, L1_conv_b_out, L1_conv_ln_scale)
    t = _to_tokens(x)
    t = t + _L2_attn_ref(_ln_t(t), L2_attn_Wq, L2_attn_bq, L2_attn_Wk, L2_attn_bk, L2_attn_Wv, L2_attn_bv)
    t = t + _L2_ffn_ref(_ln_t(t), L2_ffn_gate_w, L2_ffn_gate_b, L2_ffn_weight1, L2_ffn_weight2)
    t = t + _L3_attn_ref(_ln_t(t), L3_attn_W, L3_attn_b)
    t = t + _L3_ffn_ref(_ln_t(t), L3_ffn_sigma, L3_ffn_phi, L3_ffn_M_u, L3_ffn_M_phi_plus, L3_ffn_M_phi_minus, L3_ffn_log_weights, L3_ffn_gumbel)
    x = _from_tokens(t, x)
    return x


_drawn_inputs = setup_inputs


def setup_inputs(seed=0):
    import zlib

    import numpy as np

    out = dict(_drawn_inputs(seed))
    spreads = {'L1_conv_ln_scale': (1.0, 0.2),
     'L2_attn_bq': (0.0, 0.1),
     'L2_attn_bk': (0.0, 0.1),
     'L2_attn_bv': (0.0, 0.1),
     'L2_ffn_gate_b': (0.0, 2.0),
     'L3_ffn_log_weights': (1.0, 0.2)}
    factors = {'L0_conv_b_qkv': 8.0,
     'L0_conv_b_dw': 4.66,
     'L0_conv_pconv_off_w': 8.0,
     'L0_conv_w_off': 8.0,
     'L0_conv_b_off': 39.409,
     'L0_conv_pconv_mask_w': 8.0,
     'L1_conv_w_qkv': 8.0,
     'L1_conv_w_out': 8.0,
     'L2_ffn_gate_w': 64.0,
     'L2_ffn_weight1': 64.0,
     'L2_ffn_weight2': 64.0,
     'L3_attn_W': 200.0,
     'L3_attn_b': 200.0,
     'L3_ffn_sigma': 50.214,
     'L3_ffn_phi': 8.0,
     'L3_ffn_M_u': 200.0,
     'L3_ffn_M_phi_plus': 8.0,
     'L3_ffn_M_phi_minus': 21.74,
     'L3_ffn_gumbel': 8.0}
    for name, (base, spread) in spreads.items():
        noise = np.random.default_rng([zlib.crc32(name.encode()), seed]).standard_normal(out[name].shape)
        drawn = base * np.exp(spread * noise) if base else spread * noise
        out[name] = jnp.asarray(drawn.astype(out[name].dtype))
    for name, factor in factors.items():
        out[name] = (out[name] * factor).astype(out[name].dtype)
    return out
```

```python
from contextlib import ExitStack

import numpy as np

import concourse.bass as bass
from concourse import mybir

F32 = mybir.dt.float32
F32R = mybir.dt.float32r
U32 = mybir.dt.uint32
I32 = mybir.dt.int32
ALU = mybir.AluOpType
ACT = mybir.ActivationFunctionType
AX = mybir.AxisListType.X

P = 128
BATCH, H, W, C = 4, 64, 64, 128
N = H * W
NT = N // P
GROUPS, HC, TAPS = 4, 32, 9
GT = GROUPS * TAPS
CORNERS = 4
TH = H + 1
REC = CORNERS * 2 * HC
PH = H + 2
NG = N // 512
OFFS = 2 * GT + TAPS
QUERY = GT + GT * CORNERS
META = QUERY + C
SIZES = 4
FILTERS, LAGS = 16, 3
CH = 64
DELTA = 2 * CH - 1
FREQ = 64


def bcast(row, n):
    return row.unsqueeze(0).broadcast_to([n, row.shape[0]])


class Stage:

    passed = None

    def __init__(self, nc, ctx, name):
        self.nc, self.ctx, self.name, self.sems = nc, ctx, name, []
        ctx.callback(self.close)

    def close(self):
        if self.sems:
            self.nc.all_engine_barrier()
            self.nc.clear_and_free_semaphores(self.sems)
            self.nc.all_engine_barrier()

    def gates(self):
        if Stage.passed is None or Stage.passed[0] is not self.nc:
            Stage.passed = (self.nc, self.nc.alloc_semaphore("passed"))
        return [Stage.passed[1]] * 5

    def sb(self, name, shape, dt=F32):
        return self.ctx.enter_context(self.nc.sbuf_tensor(f"{self.name}_{name}", shape, dt))

    def psum(self, name, shape):
        return self.ctx.enter_context(self.nc.psum_tensor(f"{self.name}_{name}", shape, F32))

    def sem(self, name):
        self.sems.append(self.nc.alloc_semaphore(f"{self.name}_{name}"))
        return self.sems[-1]


class Chain:

    def __init__(self, eng, sem, gate, base=0):
        self.eng, self.sem, self.gate, self.base, self.n = eng, sem, gate, base, 0

    def __call__(self, instruction):
        self.n += 1
        instruction.then_inc(self.sem, 1)
        hold(self.eng, self.sem, self.base + self.n, self.gate)


def hold(eng, sem, value, gate):
    eng.wait_ge(sem, value)
    if not isinstance(value, int):
        eng.sem_inc(gate, 1)


def inverse_root(dve, step, root, var, scratch):
    step(dve.reciprocal(root, root))
    step(dve.tensor_tensor(scratch, root, root, ALU.mult))
    step(dve.tensor_tensor(scratch, scratch, var, ALU.mult))
    step(dve.tensor_scalar(scratch, scratch, -0.5, 1.5, ALU.mult, ALU.add))
    step(dve.tensor_tensor(root, root, scratch, ALU.mult))


def token_norm(dve, step, gate, src, dst, stats, mv, ve, root, scratch, eps, s_var, s_std, round_):
    for t in range(NT):
        ins = dve.bn_stats(stats[:, t, :], src[:, t, :])
    step(ins)
    for t in range(NT):
        ins = dve.bn_aggr(mv[:, t, :], stats[:, t, :])
    step(ins)
    step(dve.tensor_scalar(ve, mv[:, :, 1], eps, None, ALU.add))
    dve.sem_inc(s_var, 1)
    hold(dve, s_std, round_, gate)
    inverse_root(dve, step, root, ve, scratch)
    for t in range(NT):
        ins = dve.tensor_scalar(dst[:, t, :], src[:, t, :], mv[:, t, 0:1], root[:, t:t + 1], ALU.subtract, ALU.mult)
    step(ins)


def project_and_sample_points(nc, x, w_qkv, b_qkv, w_dw, b_dw, pconv_off, pconv_mask, w_off, b_off, w_mask, b_mask,
                              ident, gmean, cy, cx, ctile, base, records, meta):
    with ExitStack() as ctx:
        st = Stage(nc, ctx, "l0a")
        tok = st.sb("tok", [P, NT, C])
        chan = st.sb("chan", [P, N])
        pad_k = st.sb("pad_k", [P, PH, PH])
        pad_v = st.sb("pad_v", [P, PH, PH])
        kv_c = st.sb("kv_c", [P, 2, N])
        kv_t = st.sb("kv_t", [P, NT, GROUPS, 2, HC])
        row = st.sb("row", [P, NT, META])
        off = st.sb("off", [P, NT, OFFS])
        cy_s = st.sb("cy", [P, GT])
        ct_s = st.sb("ct", [P, NT])
        cx_s = st.sb("cx", [P, GT])
        base_s = st.sb("base", [P, GT])
        id_s = st.sb("id", [P, P])
        gm_s = st.sb("gm", [P, P])
        wq_s = st.sb("wq", [P, 3 * C])
        wn_s = st.sb("wn", [P, 3 * C])
        bq_s = st.sb("bq", [P, 3])
        bn_s = st.sb("bn", [P, 3])
        wd_s = st.sb("wd", [P, 3, TAPS])
        bd_s = st.sb("bd", [P, 3])
        wp_s = st.sb("wp", [3 * HC, 3, P + HC])
        wa_s = st.sb("wa", [P, OFFS])
        wb_s = st.sb("wb", [HC, OFFS])
        wc_s = st.sb("wc", [P, OFFS])
        bo_s = st.sb("bo", [P, OFFS])
        stats = st.sb("stats", [P, NG, 6])
        mv = st.sb("mv", [P, 2])
        m2 = st.sb("m2", [P, 2])
        sc = st.sb("sc", [P, 6])
        ps = [st.psum(f"ps{i}", [P, 512]) for i in range(6)]
        ps_s = st.psum("pss", [P, 8])

        s_const = st.sem("const")
        s_zero = st.sem("zero")
        s_border = st.sem("border")
        s_x = st.sem("x")
        s_job = st.sem("job")
        s_act = st.sem("act")
        s_offs = st.sem("offs")
        s_stat = st.sem("stat")
        s_gsum = st.sem("gsum")
        s_nm = st.sem("nm")
        s_var = st.sem("var")
        s_std = st.sem("std")
        s_bias = st.sem("bias")
        s_norm = st.sem("norm")
        s_dw = st.sem("dw")
        s_edge = st.sem("edge")
        s_shift = st.sem("shift")
        s_point = st.sem("point")
        s_sig = st.sem("sig")
        s_meta = st.sem("meta")
        s_store = st.sem("store")
        s_rec = st.sem("rec")
        s_dve = st.sem("dve")
        s_gate = st.gates()

        conv4 = tok[:, :, :].rearrange("p t c -> p (t c)")
        convm = chan[0:HC, :]
        kv_flat = kv_c[:, :, :].rearrange("p a n -> p (a n)")

        def tmp(i):
            return kv_flat[:, i * NT * GT:(i + 1) * NT * GT].rearrange("p (t k) -> p t k", k=GT)

        def itmp(i):
            return tmp(i).bitcast(I32)

        jobs = [("x", g, "act") for g in range(NG)]
        jobs += [("qkv", (f, g), "act") for f in (1, 2, 0) for g in range(NG)]
        jobs += [("kt", g, "act") for g in range(NG)] + [("vt", g, "act") for g in range(NG)]
        jobs += [("qt", g, "act") for g in range(NG)]
        jobs += [(kind, g, "act") for g in range(NG) for kind in ("off4", "offm")]
        jobs += [("offs", g, "dve") for g in range(NG)]
        NJ = len(jobs)
        n_act = [sum(1 for j in jobs[:i] if j[2] == "act") for i in range(NJ + 1)]
        NA, NV = n_act[NJ], NJ - n_act[NJ]
        NB = len(ps)
        DVE_STEPS = 67
        CONSTS = 21 * 16
        RECS = 33 * 16

        block = ctx.enter_context(nc.Block())

        @block.sync
        def _(sp):
            for dst, src in ((id_s, ident), (gm_s, gmean), (wq_s, w_qkv), (cx_s, cx), (base_s, base)):
                sp.dma_start(dst[:, :], src).then_inc(s_const, 16)
            sp.dma_start(cy_s[:, :], cy).then_inc(s_const, 16)
            sp.dma_start(ct_s[:, :], ctile).then_inc(s_const, 16)
            sp.dma_start(bq_s[:, :], b_qkv).then_inc(s_const, 16)
            sp.dma_start(bd_s[:, :], b_dw).then_inc(s_const, 16)
            sp.dma_start(wd_s[:, :, :], w_dw.rearrange("(f p) k -> p f k", p=P)).then_inc(s_const, 16)
            sp.dma_start(wp_s[:, :, 0:P], pconv_off).then_inc(s_const, 16)
            sp.dma_start(wp_s[:, :, P:P + HC], pconv_mask).then_inc(s_const, 16)
            sp.dma_start(bo_s[:, 0:2 * GT], bcast(b_off, P)).then_inc(s_const, 16)
            sp.dma_start(bo_s[:, 2 * GT:OFFS], bcast(b_mask, P)).then_inc(s_const, 16)
            sp.wait_ge(s_zero, 6)
            for g in range(GROUPS):
                sp.dma_start(wa_s[HC * g:HC * g + HC, 18 * g:18 * g + 18], w_off[0:HC, g, :]).then_inc(s_const, 16)
            sp.dma_start(wb_s[:, 2 * GT:OFFS], w_mask[0:HC, :]).then_inc(s_const, 16)
            sp.dma_start(wc_s[HC:P, 0:2 * GT].rearrange("p (g k) -> p g k", g=GROUPS), w_off[HC:P, :, :]).then_inc(s_const, 16)
            sp.dma_start(wc_s[HC:P, 2 * GT:OFFS], w_mask[HC:P, :]).then_inc(s_const, 16)
            zeros = kv_c[0:BATCH * GROUPS, :, :].rearrange("p a n -> p (a n)")
            for yi, c0 in ((0, 0), (TH - 1, 2)):
                sp.dma_start(records[:, :, yi, :, c0:c0 + 2, :].rearrange("b g x c d -> (b g) x (c d)"),
                             zeros[:, 0:128].rearrange("p (o d) -> p o d", o=1).broadcast_to([16, TH, 128])).then_inc(s_store, 16)
            sp.wait_ge(s_store, 32)
            for xi, cs in ((0, (0, 2)), (TH - 1, (1, 3))):
                for c in cs:
                    sp.dma_start(records[:, :, :, xi, c, :].rearrange("b g y d -> (b g) y d"),
                                 zeros[:, 0:64].rearrange("p (o d) -> p o d", o=1).broadcast_to([16, TH, 64])).then_inc(s_store, 16)
            with sp.Fori(0, BATCH) as b:
                hold(sp, s_offs, b * NG + 1, s_gate[0])
                tiles = x[bass.ds(b, 1), :, :].rearrange("o (t p) c -> (o p) t c", p=P)
                for h in range(0, P, P // 2):
                    sp.dma_start(tok[h:h + P // 2, :, :], tiles[h:h + P // 2, :, :]).then_inc(s_x, 16)
                hold(sp, s_act, b * NA + 6 * NG, s_gate[0])
                for half in range(2):
                    for dy in range(2):
                        for dx in range(2):
                            for g in range(GROUPS):
                                y0 = 1 - dy + half
                                dst = records[bass.ds(b, 1), g, y0:y0 + H - 1:2, 1 - dx:1 - dx + W,
                                              2 * dy + dx, :].rearrange("o t x d -> (o x) t d")
                                src = kv_t[W * half:W * half + W, :, g, :, :].rearrange("p t a d -> p t (a d)")
                                sp.dma_start(dst, src).then_inc(s_rec, 16)
                hold(sp, s_dw, b * 3 + 3, s_gate[0])
                hold(sp, s_edge, b + 1, s_gate[0])
                image = kv_c[0:HC, 0, :].rearrange("p (a b) -> p a b", b=W)
                for j in range(3):
                    lost = max(0, j - 1)
                    sp.dma_start(pad_v[HC * j:HC * j + HC, 1:1 + H, 1 - j + lost:1 - j + W], image[:, :, lost:W]).then_inc(s_shift, 16)
                hold(sp, s_meta, b + 1, s_gate[0])
                hold(sp, s_act, (b + 1) * NA, s_gate[0])
                sp.dma_start(meta[bass.ds(b, 1), :, :, :].rearrange("o t p m -> (o p) t m"), row[:, :, :]).then_inc(s_rec, 16)
                hold(sp, s_rec, (b + 1) * RECS + 1, s_gate[0])
            sp.wait_ge(s_store, 16 * (6))

        @block.gpsimd
        def _(pool):
            pool.memset(pad_k[:, :, :], 0.0).then_inc(s_zero, 1)
            pool.memset(pad_v[:, :, :], 0.0).then_inc(s_zero, 1)
            pool.memset(wa_s[:, :], 0.0).then_inc(s_zero, 1)
            pool.memset(wb_s[:, :], 0.0).then_inc(s_zero, 1)
            pool.memset(wc_s[:, :], 0.0).then_inc(s_zero, 1)
            pool.memset(kv_c[:, :, :], 0.0).then_inc(s_zero, 1)
            pool.wait_ge(s_zero, 6)
            with pool.Fori(0, BATCH) as b:
                hold(pool, s_offs, b * NG + 1, s_gate[1])
                pool.memset(pad_v[:, 0, :], 0.0).then_inc(s_border, 1)
                pool.memset(pad_v[:, PH - 1, :], 0.0).then_inc(s_border, 1)
                pool.memset(pad_v[:, 1:1 + H, 0], 0.0).then_inc(s_border, 1)
                pool.memset(pad_v[:, 1:1 + H, PH - 1], 0.0).then_inc(s_border, 1)
                hold(pool, s_dw, b * 3 + 2, s_gate[1])
                pool.memset(pad_v[2 * HC:3 * HC, 1:1 + H, W - 1], 0.0).then_inc(s_edge, 1)

        @block.tensor
        def _(pe):
            pe.wait_ge(s_const, CONSTS)
            with pe.Fori(0, BATCH) as b:
                hold(pe, s_x, b * 32 + 32, s_gate[2])
                hold(pe, s_offs, b * NG + 1, s_gate[2])
                for n, (kind, at, out) in enumerate(jobs):
                    bank = ps[n % NB]
                    if n >= NB:
                        if jobs[n - NB][2] == "act":
                            hold(pe, s_act, b * NA + n_act[n - NB + 1], s_gate[2])
                        else:
                            hold(pe, s_offs, b * NG + n - NB + 1 - n_act[n - NB + 1] + 1, s_gate[2])
                    if kind == "x":
                        for t in range(4):
                            last = pe.transpose(bank[:, t * P:t * P + P], tok[:, 4 * at + t, :], id_s[:, :])
                    if kind == "qkv":
                        f, g = at
                        if n == NG:
                            hold(pe, s_stat, b + 1, s_gate[2])
                            pe.matmul(ps_s[:, 0:2], gm_s[:, :], m2[:, :], start=True, stop=True).then_inc(s_gsum, 1)
                            hold(pe, s_nm, b + 1, s_gate[2])
                            for i in range(3):
                                mm = pe.matmul(ps_s[:, 2 + i:3 + i], wq_s[:, i * P:i * P + P], sc[:, 3:4], start=True, stop=True)
                            mm.then_inc(s_bias, 1)
                            hold(pe, s_norm, 2 * b + 1, s_gate[2])
                        last = pe.matmul(bank[:, :], wn_s[:, f * P:f * P + P], chan[:, g * 512:g * 512 + 512], start=True, stop=True)
                    if kind in ("kt", "vt", "qt"):
                        if at == 0:
                            hold(pe, s_dw, b * 3 + {"kt": 1, "vt": 2, "qt": 3}[kind], s_gate[2])
                        for t in range(4):
                            i = 4 * at + t
                            src = kv_c[:, int(kind == "vt"), i * P:i * P + P]
                            last = pe.transpose(bank[:, t * P:t * P + P], src, id_s[:, :])
                    if kind in ("off4", "offm"):
                        if at == 0:
                            hold(pe, s_shift, b * 48 + 48, s_gate[2])
                        m, o = (P, 0) if kind == "off4" else (HC, P)
                        for dy in range(3):
                            last = pe.matmul(bank[0:m, :], wp_s[:, dy, o:o + m], pad_v[0:3 * HC, 8 * at + dy:8 * at + dy + 8, 0:W],
                                             start=dy == 0, stop=dy == 2)
                    if kind == "offs":
                        if at == 0:
                            hold(pe, s_act, b * NA + NA, s_gate[2])
                        for t in range(4):
                            i = 4 * at + t
                            o = bank[:, t * P:t * P + OFFS]
                            pe.matmul(o, conv4[:, i * P:i * P + P], wa_s[:, :], start=True, stop=False)
                            pe.matmul(o, convm[:, i * P:i * P + P], wb_s[:, :], start=False, stop=False)
                            last = pe.matmul(o, kv_c[:, 0, i * P:i * P + P], wc_s[:, :], start=False, stop=True)
                    last.then_inc(s_job, 1)

        @block.scalar
        def _(act):
            act.sem_inc(s_rec, 1)
            act.wait_ge(s_zero, 6)
            with act.Fori(0, BATCH) as b:
                for n, (kind, at, out) in enumerate(jobs):
                    if out != "act":
                        continue
                    if n == NG:
                        hold(act, s_var, b + 1, s_gate[3])
                        act.activation(sc[:, 2:3], sc[:, 4:5], ACT.Sqrt).then_inc(s_std, 1)
                    hold(act, s_job, b * NJ + n + 1, s_gate[3])
                    bank = ps[n % NB]
                    if kind == "x":
                        ins = act.activation(chan[:, at * 512:at * 512 + 512], bank[:, :], ACT.Copy)
                    if kind == "qkv":
                        f, g = at
                        dst = pad_v if f == 2 else pad_k
                        if g == 0 and f == 1:
                            hold(act, s_norm, 2 * b + 2, s_gate[3])
                        if g == 0 and f == 2:
                            hold(act, s_border, b * 4 + 4, s_gate[3])
                        if g == 0 and f == 0:
                            hold(act, s_dw, b * 3 + 1, s_gate[3])
                        ins = act.activation(dst[:, 1 + 8 * g:9 + 8 * g, 1:1 + W], bank[:, :].rearrange("p (a b) -> p a b", b=W),
                                             ACT.Identity, bias=bn_s[:, f:f + 1])
                    if kind in ("kt", "vt"):
                        if at == 0 and kind == "kt":
                            hold(act, s_rec, b * RECS + 1, s_gate[3])
                        ins = act.activation(kv_t[:, 4 * at:4 * at + 4, :, int(kind == "vt"), :],
                                             bank[:, :].rearrange("p (t g d) -> p t g d", g=GROUPS, d=HC), ACT.Copy)
                    if kind == "qt":
                        ins = act.activation(row[:, 4 * at:4 * at + 4, QUERY:META], bank[:, :].rearrange("p (t c) -> p t c", c=C),
                                             ACT.Copy, scale=float(HC) ** -0.5)
                    if kind == "off4":
                        ins = act.activation(conv4[:, at * 512:at * 512 + 512], bank[:, :], ACT.Copy)
                    if kind == "offm":
                        ins = act.activation(convm[:, at * 512:at * 512 + 512], bank[0:HC, :], ACT.Copy)
                    ins.then_inc(s_act, 1)
                hold(act, s_point, b + 1, s_gate[3])
                act.activation(off[:, :, 2 * GT:OFFS], off[:, :, 2 * GT:OFFS], ACT.Sigmoid).then_inc(s_sig, 1)

        @block.vector
        def _(dve):
            dve.wait_ge(s_const, CONSTS)
            dve.wait_ge(s_zero, 6)
            dve.wait_ge(s_store, 6 * 16)
            dve.sem_inc(s_offs, 1)
            with dve.Fori(0, BATCH) as b:
                step = Chain(dve, s_dve, s_gate[4], b * DVE_STEPS)
                for g in range(NG):
                    hold(dve, s_act, b * NA + g + 1, s_gate[4])
                    ins = dve.bn_stats(stats[:, g, :], chan[:, g * 512:g * 512 + 512])
                step(ins)
                step(dve.bn_aggr(mv[:, :], stats[:, :, :].rearrange("p a b -> p (a b)")))
                step(dve.tensor_tensor(m2[:, 1:2], mv[:, 0:1], mv[:, 0:1], ALU.mult))
                step(dve.tensor_tensor(m2[:, 1:2], m2[:, 1:2], mv[:, 1:2], ALU.add))
                dve.tensor_copy(m2[:, 0:1], mv[:, 0:1]).then_inc(s_stat, 1)
                hold(dve, s_gsum, b + 1, s_gate[4])
                step(dve.tensor_copy(sc[:, 0:2], ps_s[:, 0:2]))
                step(dve.tensor_tensor(sc[:, 2:3], sc[:, 0:1], sc[:, 0:1], ALU.mult))
                step(dve.tensor_tensor(sc[:, 2:3], sc[:, 1:2], sc[:, 2:3], ALU.subtract))
                step(dve.tensor_scalar(sc[:, 4:5], sc[:, 2:3], 1e-5, None, ALU.add))
                dve.sem_inc(s_var, 1)
                hold(dve, s_std, b + 1, s_gate[4])
                inverse_root(dve, step, sc[:, 2:3], sc[:, 4:5], sc[:, 5:6])
                dve.scalar_tensor_tensor(sc[:, 3:4], sc[:, 0:1], -1.0, sc[:, 2:3], ALU.mult, ALU.mult).then_inc(s_nm, 1)
                dve.tensor_scalar(wn_s[:, :], wq_s[:, :], sc[:, 2:3], None, ALU.mult).then_inc(s_norm, 1)
                hold(dve, s_bias, b + 1, s_gate[4])
                dve.tensor_tensor(bn_s[:, :], ps_s[:, 2:5], bq_s[:, :], ALU.add).then_inc(s_norm, 1)
                for i, f in enumerate((1, 2, 0)):
                    src = pad_v if f == 2 else pad_k
                    dst = kv_c[:, int(f == 2), :].rearrange("p (a b) -> p a b", b=W)
                    if f == 0:
                        hold(dve, s_job, b * NJ + 5 * NG, s_gate[4])
                    hold(dve, s_act, b * NA + (2 + i) * NG, s_gate[4])
                    for t in range(TAPS):
                        win = src[:, t // 3:t // 3 + H, t % 3:t % 3 + W]
                        if t == 0:
                            step(dve.tensor_scalar(dst, win, wd_s[:, f, 0:1], bd_s[:, f:f + 1], ALU.mult, ALU.add))
                        else:
                            step(dve.scalar_tensor_tensor(dst, win, wd_s[:, f, t:t + 1], dst, ALU.mult, ALU.add))
                    dve.sem_inc(s_dw, 1)
                for g in range(NG):
                    n = NJ - NG + g
                    hold(dve, s_job, b * NJ + n + 1, s_gate[4])
                    dve.tensor_tensor(off[:, 4 * g:4 * g + 4, :], ps[n % NB][:, :].rearrange("p (t k) -> p t k", k=P)[:, :, 0:OFFS],
                                      bo_s[:, :].unsqueeze(1).broadcast_to([P, 4, OFFS]), ALU.add).then_inc(s_offs, 1)
                hold(dve, s_offs, b * NG + NG + 1, s_gate[4])
                offv = off[:, :, 0:2 * GT].rearrange("p t (k a) -> p t k a", a=2)
                py, px, whole, above, y0, x0 = (tmp(i) for i in range(6))
                step(dve.tensor_tensor(py, offv[:, :, :, 0], cy_s[:, :].unsqueeze(1).broadcast_to([P, NT, GT]), ALU.add))
                step(dve.tensor_tensor(py, py, ct_s[:, :].unsqueeze(2).broadcast_to([P, NT, GT]), ALU.add))
                step(dve.tensor_tensor(px, offv[:, :, :, 1], cx_s[:, :].unsqueeze(1).broadcast_to([P, NT, GT]), ALU.add))
                dve.sem_inc(s_point, 1)
                for pos, cell in ((py, y0), (px, x0)):
                    step(dve.tensor_scalar(pos, pos, -1.0, float(H), ALU.max, ALU.min))
                    step(dve.tensor_copy(whole.bitcast(I32), pos))
                    step(dve.tensor_copy(cell, whole.bitcast(I32)))
                    step(dve.tensor_tensor(above, cell, pos, ALU.is_gt))
                    step(dve.tensor_tensor(cell, cell, above, ALU.subtract))
                    step(dve.tensor_scalar(cell, cell, float(H - 1), None, ALU.min))
                    step(dve.tensor_tensor(pos, pos, cell, ALU.subtract))
                step(dve.scalar_tensor_tensor(y0, y0, float(TH), x0, ALU.mult, ALU.add))
                step(dve.tensor_tensor(y0, y0, base_s[:, :].unsqueeze(1).broadcast_to([P, NT, GT]), ALU.add))
                step(dve.tensor_copy(row[:, :, 0:GT].bitcast(U32), y0))
                step(dve.tensor_scalar(base_s[:, :], base_s[:, :], float(GROUPS * TH * TH), None, ALU.add))
                hold(dve, s_sig, b + 1, s_gate[4])
                mask = off[:, :, 2 * GT:OFFS].unsqueeze(2).broadcast_to([P, NT, GROUPS, TAPS])
                lower, upper = whole, above
                wgt = row[:, :, GT:QUERY].rearrange("p t (k c) -> p t k c", c=CORNERS)
                step(dve.tensor_tensor(lower.rearrange("p t (g k) -> p t g k", k=TAPS), mask,
                                       py.rearrange("p t (g k) -> p t g k", k=TAPS), ALU.mult))
                step(dve.tensor_tensor(upper.rearrange("p t (g k) -> p t g k", k=TAPS), mask,
                                       lower.rearrange("p t (g k) -> p t g k", k=TAPS), ALU.subtract))
                for i, part in enumerate((upper, lower)):
                    step(dve.tensor_tensor(wgt[:, :, :, 2 * i + 1], part, px, ALU.mult))
                    step(dve.tensor_tensor(wgt[:, :, :, 2 * i], part, wgt[:, :, :, 2 * i + 1], ALU.subtract))
                dve.sem_inc(s_meta, 1)
                assert step.n == DVE_STEPS, step.n


def sample_and_attend(nc, x, records, meta, w_proj, b_proj, ident, out):
    with ExitStack() as ctx:
        st = Stage(nc, ctx, "l0b")
        row = [st.sb(f"row{i}", [P, META]) for i in range(2)]
        rec = [st.sb(f"rec{i}", [P, GT, REC]) for i in range(2)]
        res = [st.sb(f"res{i}", [P, C]) for i in range(2)]
        fin = [st.sb(f"fin{i}", [P, C]) for i in range(2)]
        prod_k = st.sb("prod_k", [P, GT * CORNERS, HC])
        prod_v = [st.sb(f"prod_v{i}", [P, TAPS * CORNERS, GROUPS, HC]) for i in range(2)]
        dots = st.sb("dots", [P, GT, CORNERS])
        score = st.sb("score", [P, GT])
        prob = st.sb("prob", [P, GT])
        peak = st.sb("peak", [P, GROUPS])
        total = st.sb("total", [P, GROUPS])
        att_c = st.sb("att_c", [P, P])
        id_s = st.sb("id", [P, P])
        wp_s = st.sb("wp", [P, C])
        bp_s = st.sb("bp", [1, C])
        ones = st.sb("ones", [1, P])
        ps_a = st.psum("psa", [P, P])
        ps_p = st.psum("psp", [P, C])
        s_const = st.sem("const")
        s_ones = st.sem("ones")
        s_row = [st.sem(f"row{i}") for i in range(2)]
        s_rec = [st.sem(f"rec{i}") for i in range(2)]
        s_fin = [st.sem(f"fin{i}") for i in range(2)]
        s_free = st.sem("free")
        s_score = st.sem("score")
        s_exp = st.sem("exp")
        s_pv = st.sem("pv")
        s_att = st.sem("att")
        s_attc = st.sem("attc")
        s_proj = st.sem("proj")
        s_out = st.sem("out")
        s_dve = st.sem("dve")
        s_gate = st.gates()
        DVE_STEPS = 12
        block = ctx.enter_context(nc.Block())

        @block.sync
        def _(sp):
            sp.dma_start(id_s[:, :], ident).then_inc(s_const, 16)
            sp.dma_start(wp_s[:, :], w_proj).then_inc(s_const, 16)
            sp.dma_start(bp_s[:, :], b_proj).then_inc(s_const, 16)
            with sp.Fori(0, BATCH * NT // 2) as i:
                for s in range(2):
                    t = 2 * i + s
                    hold(sp, s_out, t + 1, s_gate[0])
                    sp.dma_start(row[s][:, :], meta[bass.ds(t, 1), :, :].rearrange("o p m -> (o p) m")).then_inc(s_row[s], 16)
                    sp.dma_start(res[s][:, :], x[bass.ds(t, 1), :, :].rearrange("o p c -> (o p) c")).then_inc(s_row[s], 16)

        @block.gpsimd
        def _(pool):
            with pool.Fori(0, BATCH * NT // 2) as i:
                for s in range(2):
                    hold(pool, s_row[s], 32 * i + 32, s_gate[1])
                    hold(pool, s_free, 2 * i + s + 1, s_gate[1])
                    for k in range(GT):
                        pool.indirect_dma_start(out=rec[s][:, k, :], out_offset=None, in_=records,
                                                in_offset=bass.IndirectOffsetOnAxis(ap=row[s][:, k:k + 1].bitcast(U32), axis=0)
                                                ).then_inc(s_rec[s], 16)

        @block.vector
        def _(dve):
            dve.memset(ones[:, :], 1.0).then_inc(s_ones, 1)
            dve.sem_inc(s_free, 2)
            dve.sem_inc(s_out, 2)
            dve.sem_inc(s_att, 2)
            with dve.Fori(0, BATCH * NT // 2) as i:
                for s in range(2):
                    t = 2 * i + s
                    step = Chain(dve, s_dve, s_gate[2], t * DVE_STEPS)
                    view = rec[s][:, :, :].rearrange("p (g k) (c d) -> p g (k c) d", k=TAPS, c=CORNERS)
                    query = row[s][:, QUERY:META].rearrange("p (g o d) -> p g o d", o=1, d=HC)
                    pk = prod_k[:, :, :].rearrange("p (g m) d -> p g m d", g=GROUPS)
                    wgt = row[s][:, GT:QUERY]
                    hold(dve, s_rec[s], 16 * GT * i + 16 * GT, s_gate[2])
                    step(dve.tensor_tensor(pk, view[:, :, :, 0:HC], query.broadcast_to([P, GROUPS, TAPS * CORNERS, HC]), ALU.mult))
                    flat = dots[:, :, :].rearrange("p k c -> p (k c)")
                    step(dve.tensor_reduce(flat, prod_k[:, :, :], AX, ALU.add))
                    step(dve.tensor_tensor(flat, flat, wgt, ALU.mult))
                    step(dve.tensor_reduce(score[:, :], dots[:, :, :], AX, ALU.add))
                    sg = score[:, :].rearrange("p (g k) -> p g k", k=TAPS)
                    pg = prob[:, :].rearrange("p (g k) -> p g k", k=TAPS)
                    step(dve.tensor_reduce(peak[:, :], sg, AX, ALU.max))
                    step(dve.tensor_tensor(sg, sg, peak[:, :].unsqueeze(2).broadcast_to([P, GROUPS, TAPS]), ALU.subtract))
                    dve.sem_inc(s_score, 1)
                    hold(dve, s_exp, t + 1, s_gate[2])
                    step(dve.tensor_reduce(total[:, :], pg, AX, ALU.add))
                    step(dve.reciprocal(total[:, :], total[:, :]))
                    step(dve.tensor_tensor(pg, pg, total[:, :].unsqueeze(2).broadcast_to([P, GROUPS, TAPS]), ALU.mult))
                    step(dve.tensor_tensor(dots[:, :, :], wgt.rearrange("p (k c) -> p k c", c=CORNERS),
                                           prob[:, :].unsqueeze(2).broadcast_to([P, GT, CORNERS]), ALU.mult))
                    hold(dve, s_att, t + 1, s_gate[2])
                    pv = prod_v[s][:, :, :, :].rearrange("p m g d -> p g m d")
                    step(dve.tensor_tensor(pv, view[:, :, :, HC:2 * HC],
                                           dots[:, :, :].rearrange("p (g k) c -> p g (k c)", k=TAPS).unsqueeze(3).broadcast_to(
                                               [P, GROUPS, TAPS * CORNERS, HC]), ALU.mult))
                    dve.sem_inc(s_pv, 1)
                    dve.sem_inc(s_free, 1)
                    hold(dve, s_proj, t + 1, s_gate[2])
                    step(dve.tensor_tensor(fin[s][:, :], ps_p[:, :], res[s][:, :], ALU.add))
                    dve.sem_inc(s_out, 1)
                    assert step.n == DVE_STEPS, step.n

        @block.scalar
        def _(act):
            with act.Fori(0, BATCH * NT // 2) as i:
                for s in range(2):
                    t = 2 * i + s
                    hold(act, s_score, t + 1, s_gate[3])
                    act.activation(prob[:, :], score[:, :], ACT.Exp).then_inc(s_exp, 1)
                    hold(act, s_att, t + 3, s_gate[3])
                    act.activation(att_c[:, :], ps_a[:, :], ACT.Copy).then_inc(s_attc, 1)
                    hold(act, s_out, t + 3, s_gate[3])
                    act.dma_start(out[bass.ds(t, 1), :, :].rearrange("o p c -> (o p) c"), fin[s][:, :]).then_inc(s_fin[s], 16)
                    hold(act, s_fin[s], 16 * i + 16, s_gate[3])

        @block.tensor
        def _(pe):
            pe.wait_ge(s_const, 48)
            pe.wait_ge(s_ones, 1)
            with pe.Fori(0, BATCH * NT // 2) as i:
                for s in range(2):
                    t = 2 * i + s
                    hold(pe, s_pv, t + 1, s_gate[4])
                    for m in range(TAPS * CORNERS):
                        mm = pe.matmul(ps_a[:, :], prod_v[s][:, m, :, :].rearrange("p g d -> p (g d)"), id_s[:, :], start=m == 0, stop=m == TAPS * CORNERS - 1)
                    mm.then_inc(s_att, 1)
                    hold(pe, s_attc, t + 1, s_gate[4])
                    pe.matmul(ps_p[:, :], att_c[:, :], wp_s[:, :], start=True, stop=False)
                    pe.matmul(ps_p[:, :], ones[:, :], bp_s[:, :], start=False, stop=True).then_inc(s_proj, 1)


def linear_attention_layer(nc, x, w_qkv, w_out, b_out, ln_scale, ident, gmean, out):
    with ExitStack() as ctx:
        st = Stage(nc, ctx, "l1")
        tok = st.sb("tok", [P, NT, C])
        chan = st.sb("chan", [P, N])
        k_c = st.sb("k_c", [P, N])
        k_t = st.sb("k_t", [P, NT, C])
        qv = st.sb("qv", [P, NT, 2, C])
        fin = st.sb("fin", [P, NT, C])
        id_s = st.sb("id", [P, P])
        gm_s = st.sb("gm", [P, P])
        w_s = st.sb("w", [P, 3, C])
        wn_s = st.sb("wn", [P, 3, C])
        wo_s = st.sb("wo", [P, C])
        bo_s = st.sb("bo", [1, C])
        ls_s = st.sb("ls", [P, C])
        ones = st.sb("ones", [1, P])
        brow = st.sb("brow", [1, 3, C])
        bcol = st.sb("bcol", [P, 1])
        stats = st.sb("stats", [P, NG, 6])
        mv = st.sb("mv", [P, 2])
        m2 = st.sb("m2", [P, 2])
        sc = st.sb("sc", [P, 6])
        kmax = st.sb("kmax", [P, 1])
        ksum = st.sb("ksum", [P, 1])
        hmax = st.sb("hmax", [P, NT * 4])
        hsum = st.sb("hsum", [P, NT * 4])
        blocks = st.sb("blocks", [P, P])
        mix = st.sb("mix", [P, C])
        lst = st.sb("lst", [P, NT, 6])
        lmv = st.sb("lmv", [P, NT, 2])
        lve = st.sb("lve", [P, NT])
        lrt = st.sb("lrt", [P, NT])
        lsc = st.sb("lsc", [P, NT])
        ps = [st.psum(f"ps{i}", [P, 512]) for i in range(6)]
        ps_s = st.psum("pss", [P, 512])
        ps_c = st.psum("psc", [P, 512])

        s_const = st.sem("const")
        s_zero = st.sem("zero")
        s_x = st.sem("x")
        s_job = st.sem("job")
        s_act = st.sem("act")
        s_stat = st.sem("stat")
        s_gsum = st.sem("gsum")
        s_var = st.sem("var")
        s_std = st.sem("std")
        s_nm = st.sem("nm")
        s_bias = st.sem("bias")
        s_norm = st.sem("norm")
        s_kmax = st.sem("kmax")
        s_kexp = st.sem("kexp")
        s_qmax = st.sem("qmax")
        s_qexp = st.sem("qexp")
        s_qdone = st.sem("qdone")
        s_ctx = st.sem("ctx")
        s_blk = st.sem("blk")
        s_mix = st.sem("mix")
        s_mixc = st.sem("mixc")
        s_lvar = st.sem("lvar")
        s_lstd = st.sem("lstd")
        s_fin = st.sem("fin")
        s_out = st.sem("out")
        s_dve = st.sem("dve")
        s_gate = st.gates()

        jobs = [("x", g) for g in range(NG)] + [("k", g) for g in range(NG)] + [("qv", g) for g in range(2 * NG)]
        jobs += [("kt", g) for g in range(NG)] + [("qt", g) for g in range(NG)] + [("o", g) for g in range(NG)]
        NJ, NB = len(jobs), len(ps)
        FIRST = {kind: min(n for n, j in enumerate(jobs) if j[0] == kind) for kind, _ in jobs}
        DVE_STEPS = 34
        block = ctx.enter_context(nc.Block())

        @block.sync
        def _(sp):
            for dst, src in ((id_s, ident), (gm_s, gmean), (wo_s, w_out), (bo_s, b_out), (ls_s, bcast(ln_scale, P))):
                sp.dma_start(dst[:, :], src).then_inc(s_const, 16)
            sp.dma_start(w_s[:, :, :], w_qkv.rearrange("c (f d) -> c f d", d=C)).then_inc(s_const, 16)
            sp.sem_inc(s_out, 1)
            with sp.Fori(0, BATCH) as b:
                hold(sp, s_out, b * 32 + 1, s_gate[0])
                tiles = x[bass.ds(b, 1), :, :].rearrange("o (t p) c -> (o p) t c", p=P)
                for h in range(0, P, P // 2):
                    sp.dma_start(tok[h:h + P // 2, :, :], tiles[h:h + P // 2, :, :]).then_inc(s_x, 16)
                hold(sp, s_fin, b + 1, s_gate[0])
                res = out[bass.ds(b, 1), :, :].rearrange("o (t p) c -> (o p) t c", p=P)
                for h in range(0, P, P // 2):
                    sp.dma_start(res[h:h + P // 2, :, :], fin[h:h + P // 2, :, :]).then_inc(s_out, 16)
            sp.wait_ge(s_out, BATCH * 32 + 1)

        @block.tensor
        def _(pe):
            pe.wait_ge(s_const, 6 * 16)
            pe.wait_ge(s_zero, 2)
            with pe.Fori(0, BATCH) as b:
                hold(pe, s_x, b * 32 + 32, s_gate[1])
                hold(pe, s_act, b * NJ + 1, s_gate[1])
                for n, (kind, g) in enumerate(jobs):
                    bank = ps[n % NB]
                    if n >= NB:
                        hold(pe, s_act, b * NJ + n - NB + 2, s_gate[1])
                    if kind == "x":
                        for t in range(4):
                            last = pe.transpose(bank[:, t * P:t * P + P], tok[:, 4 * g + t, :], id_s[:, :])
                    if kind == "k":
                        if g == 0:
                            hold(pe, s_stat, b + 1, s_gate[1])
                            pe.matmul(ps_s[:, 0:2], gm_s[:, :], m2[:, :], start=True, stop=True).then_inc(s_gsum, 1)
                            hold(pe, s_nm, b + 1, s_gate[1])
                            pe.matmul(ps_s[:, 2:3], w_s[:, 1, :], sc[:, 3:4], start=True, stop=True)
                            pe.matmul(ps_s[0:1, 128:512], sc[:, 3:4], w_s[:, :, :].rearrange("p f d -> p (f d)"),
                                      start=True, stop=True).then_inc(s_bias, 1)
                            hold(pe, s_norm, b * 3 + 3, s_gate[1])
                        last = pe.matmul(bank[:, :], wn_s[:, 1, :], chan[:, g * 512:g * 512 + 512], start=True, stop=True)
                    if kind == "qv":
                        for t in range(2):
                            o = bank[:, t * 256:t * 256 + 256].rearrange("p (f d) -> p f d", f=2)
                            i = 2 * g + t
                            pe.matmul(o, chan[:, i * P:i * P + P], wn_s[:, 0:3:2, :], start=True, stop=False)
                            last = pe.matmul(o, ones[:, :], brow[:, 0:3:2, :], start=False, stop=True)
                    if kind == "kt":
                        if g == 0:
                            hold(pe, s_kexp, b + 1, s_gate[1])
                        for t in range(4):
                            i = 4 * g + t
                            last = pe.transpose(bank[:, t * P:t * P + P], k_c[:, i * P:i * P + P], id_s[:, :])
                    if kind == "qt":
                        if g == 0:
                            hold(pe, s_act, b * NJ + FIRST["qt"] + 1, s_gate[1])
                            for t in range(NT):
                                mm = pe.matmul(ps_c[:, 0:P], qv[:, t, 1, :], k_t[:, t, :], start=t == 0, stop=t == NT - 1)
                            mm.then_inc(s_ctx, 1)
                            hold(pe, s_qdone, b + 1, s_gate[1])
                        for t in range(4):
                            i = 4 * g + t
                            last = pe.transpose(bank[:, t * P:t * P + P], qv[:, i, 0, :], id_s[:, :])
                    if kind == "o":
                        if g == 0:
                            hold(pe, s_blk, b + 1, s_gate[1])
                            pe.matmul(ps_c[:, P:2 * P], blocks[:, :], wo_s[:, :], start=True, stop=True).then_inc(s_mix, 1)
                            hold(pe, s_mixc, b + 1, s_gate[1])
                            hold(pe, s_act, b * NJ + FIRST["o"] + 1, s_gate[1])
                        for t in range(4):
                            i = 4 * g + t
                            o = bank[:, t * P:t * P + P]
                            pe.matmul(o, chan[:, i * P:i * P + P], mix[:, :], start=True, stop=False)
                            last = pe.matmul(o, ones[:, :], bo_s[:, :], start=False, stop=True)
                    last.then_inc(s_job, 1)

        @block.scalar
        def _(act):
            act.sem_inc(s_act, 1)
            with act.Fori(0, BATCH) as b:
                for n, (kind, g) in enumerate(jobs):
                    if kind == "k" and g == 0:
                        hold(act, s_var, b + 1, s_gate[2])
                        act.activation(sc[:, 2:3], sc[:, 4:5], ACT.Sqrt).then_inc(s_std, 1)
                        hold(act, s_norm, b * 3 + 3, s_gate[2])
                    if kind == "kt" and g == 0:
                        hold(act, s_kmax, b + 1, s_gate[2])
                        act.activation(k_c[:, :], k_c[:, :], ACT.Exp, bias=kmax[:, :], accum_out=ksum[:, :]).then_inc(s_kexp, 1)
                        hold(act, s_qmax, b + 1, s_gate[2])
                        act.activation(qv[:, :, 0, :], qv[:, :, 0, :], ACT.Exp).then_inc(s_qexp, 1)
                    hold(act, s_job, b * NJ + n + 1, s_gate[2])
                    bank = ps[n % NB][:, :]
                    if kind in ("x", "qt"):
                        ins = act.activation(chan[:, g * 512:g * 512 + 512], bank, ACT.Copy)
                    if kind == "k":
                        ins = act.activation(k_c[:, g * 512:g * 512 + 512], bank, ACT.Identity, bias=bcol[:, :])
                    if kind == "qv":
                        ins = act.activation(qv[:, 2 * g:2 * g + 2, :, :].rearrange("p t f d -> p (t f d)"), bank, ACT.Copy)
                    if kind in ("kt", "o"):
                        ins = act.activation(k_t[:, 4 * g:4 * g + 4, :].rearrange("p t d -> p (t d)"), bank, ACT.Copy)
                    ins.then_inc(s_act, 1)
                hold(act, s_lvar, b + 1, s_gate[2])
                act.activation(lrt[:, :], lve[:, :], ACT.Sqrt).then_inc(s_lstd, 1)

        @block.vector
        def _(dve):
            dve.memset(ones[:, :], 1.0).then_inc(s_zero, 1)
            dve.memset(blocks[:, :], 0.0).then_inc(s_zero, 1)
            dve.wait_ge(s_const, 6 * 16)
            dve.wait_ge(s_zero, 2)
            with dve.Fori(0, BATCH) as b:
                gate = s_gate[3]
                step = Chain(dve, s_dve, gate, b * DVE_STEPS)
                for g in range(NG):
                    hold(dve, s_act, b * NJ + g + 2, gate)
                    ins = dve.bn_stats(stats[:, g, :], chan[:, g * 512:g * 512 + 512])
                step(ins)
                step(dve.bn_aggr(mv[:, :], stats[:, :, :].rearrange("p a b -> p (a b)")))
                step(dve.tensor_tensor(m2[:, 1:2], mv[:, 0:1], mv[:, 0:1], ALU.mult))
                step(dve.tensor_tensor(m2[:, 1:2], m2[:, 1:2], mv[:, 1:2], ALU.add))
                dve.tensor_copy(m2[:, 0:1], mv[:, 0:1]).then_inc(s_stat, 1)
                hold(dve, s_gsum, b + 1, gate)
                step(dve.tensor_copy(sc[:, 0:2], ps_s[:, 0:2]))
                step(dve.tensor_tensor(sc[:, 2:3], sc[:, 0:1], sc[:, 0:1], ALU.mult))
                step(dve.tensor_tensor(sc[:, 2:3], sc[:, 1:2], sc[:, 2:3], ALU.subtract))
                step(dve.tensor_scalar(sc[:, 4:5], sc[:, 2:3], 1e-5, None, ALU.add))
                dve.sem_inc(s_var, 1)
                hold(dve, s_std, b + 1, gate)
                inverse_root(dve, step, sc[:, 2:3], sc[:, 4:5], sc[:, 5:6])
                dve.scalar_tensor_tensor(sc[:, 3:4], sc[:, 0:1], -1.0, sc[:, 2:3], ALU.mult, ALU.mult).then_inc(s_nm, 1)
                dve.tensor_scalar(wn_s[:, :, :], w_s[:, :, :], sc[:, 2:3], None, ALU.mult).then_inc(s_norm, 1)
                hold(dve, s_bias, b + 1, gate)
                dve.tensor_copy(bcol[:, :], ps_s[:, 2:3]).then_inc(s_norm, 1)
                dve.tensor_copy(brow[:, :, :].rearrange("p f d -> p (f d)"), ps_s[0:1, 128:512]).then_inc(s_norm, 1)
                hold(dve, s_act, b * NJ + FIRST["qv"] + 1, gate)
                step(dve.tensor_reduce(kmax[:, :], k_c[:, :], AX, ALU.max))
                step(dve.tensor_scalar(kmax[:, :], kmax[:, :], -1.0, None, ALU.mult))
                dve.sem_inc(s_kmax, 1)
                hold(dve, s_act, b * NJ + FIRST["kt"] + 1, gate)
                q = qv[:, :, 0, :].rearrange("p t (h d) -> p t h d", d=HC)
                per = [P, NT, 4, HC]
                hm = hmax[:, :].rearrange("p (t h) -> p t h", h=4)
                hs = hsum[:, :].rearrange("p (t h) -> p t h", h=4)
                step(dve.tensor_reduce(hm, q, AX, ALU.max))
                step(dve.tensor_tensor(q, q, hm.unsqueeze(3).broadcast_to(per), ALU.subtract))
                dve.sem_inc(s_qmax, 1)
                hold(dve, s_qexp, b + 1, gate)
                step(dve.tensor_reduce(hs, q, AX, ALU.add))
                step(dve.reciprocal(hsum[:, :], hsum[:, :]))
                step(dve.tensor_scalar(hsum[:, :], hsum[:, :], float(HC) ** -0.5, None, ALU.mult))
                step(dve.tensor_tensor(q, q, hs.unsqueeze(3).broadcast_to(per), ALU.mult))
                dve.sem_inc(s_qdone, 1)
                hold(dve, s_ctx, b + 1, gate)
                step(dve.reciprocal(ksum[:, :], ksum[:, :]))
                for h in range(4):
                    r = slice(HC * h, HC * h + HC)
                    ins = dve.tensor_copy(blocks[r, r], ps_c[r, r])
                step(ins)
                dve.sem_inc(s_blk, 1)
                hold(dve, s_mix, b + 1, gate)
                dve.tensor_scalar(mix[:, :], ps_c[:, P:2 * P], ksum[:, :], 1.0 / N, ALU.mult, ALU.mult).then_inc(s_mixc, 1)
                hold(dve, s_act, b * NJ + NJ + 1, gate)
                hold(dve, s_out, b * 32 + 1, gate)
                token_norm(dve, step, gate, k_t, fin, lst, lmv, lve[:, :], lrt[:, :], lsc[:, :], 1e-5, s_lvar, s_lstd, b + 1)
                step(dve.tensor_tensor(fin[:, :, :], fin[:, :, :], ls_s[:, :].unsqueeze(1).broadcast_to([P, NT, C]), ALU.mult))
                step(dve.tensor_tensor(fin[:, :, :], fin[:, :, :], tok[:, :, :], ALU.add))
                dve.sem_inc(s_fin, 1)
                assert step.n == DVE_STEPS, step.n


EXPERTS, HIDDEN = 64, 512
HCH = HIDDEN // P
EB = 8


def gate_layer(nc, x, wq_t, wk, wv, bq, bk, bv, gate_t, gate_b, ident, mid, picks, pooled):
    with ExitStack() as ctx:
        st = Stage(nc, ctx, "l2a")
        tok = st.sb("tok", [P, NT, C])
        unit = st.sb("unit", [P, 2, NT, C])
        chan = st.sb("chan", [P, N])
        k_c = st.sb("k_c", [P, N])
        logit = st.sb("logit", [P, N])
        rest = st.sb("rest", [P, N])
        id_s = st.sb("id", [P, P])
        wq_s = st.sb("wq", [P, C])
        wk_s = st.sb("wk", [P, C])
        wv_s = st.sb("wv", [P, C])
        b3_s = st.sb("b3", [P, 3])
        gw_s = st.sb("gw", [P, EXPERTS])
        gb_s = st.sb("gb", [P, 1])
        ones = st.sb("ones", [1, P])
        part = st.sb("part", [P, NG])
        kv = st.sb("kv", [P, 1])
        bkv = st.sb("bkv", [P, 1])
        diag = st.sb("diag", [P, P])
        wkv = st.sb("wkv", [P, C])
        brow = st.sb("brow", [1, C])
        scr = st.sb("scr", [P, 512])
        top = st.sb("top", [P, 8])
        peak = st.sb("peak", [P, 1])
        total = st.sb("total", [P, 1])
        lst = st.sb("lst", [P, NT, 6])
        lmv = st.sb("lmv", [P, NT, 2])
        lve = st.sb("lve", [P, NT])
        lrt = st.sb("lrt", [P, NT])
        lsc = st.sb("lsc", [P, NT])
        ps = [st.psum(f"ps{i}", [P, 512]) for i in range(6)]
        ps_s = st.psum("pss", [P, 512])

        s_const = st.sem("const")
        s_ones = st.sem("ones")
        s_x = st.sem("x")
        s_job = st.sem("job")
        s_act = st.sem("act")
        s_v = st.sem("v")
        s_var = st.sem("var")
        s_std = st.sem("std")
        s_free = st.sem("free")
        s_unit = st.sem("unit")
        s_diag = st.sem("diag")
        s_scaled = st.sem("scaled")
        s_wkv = st.sem("wkv")
        s_mid = st.sem("mid")
        s_midout = st.sem("midout")
        s_peak = st.sem("peak")
        s_exp = st.sem("exp")
        s_pick = st.sem("pick")
        s_pickout = st.sem("pickout")
        s_pool = st.sem("pool")
        s_pooled = st.sem("pooled")
        s_dve = st.sem("dve")
        s_gate = st.gates()

        jobs = []
        for h in range(2):
            jobs += [("u", h, g, "act") for g in range(NG)] + [("k", h, g, "act") for g in range(NG)]
            jobs += [("v", h, g, "dve") for g in range(NG)] + [("o", h, g, "dve") for g in range(NG)]
            jobs += [("u2", h, g, "act") for g in range(NG)] + [("log", h, g, "act") for g in range(NG)]
        jobs += [("pt", 0, g, "act") for g in range(NG)]
        NJ, NB = len(jobs), len(ps)
        NA = sum(j[3] == "act" for j in jobs)
        ND = NJ - NA

        def taken(n):
            return sum(j[3] == "act" for j in jobs[:n + 1]), sum(j[3] == "dve" for j in jobs[:n + 1])

        DVE_STEPS = 83
        block = ctx.enter_context(nc.Block())

        def tiles(dram, b):
            return dram[bass.ds(b, 1), :, :].rearrange("o (t p) c -> (o p) t c", p=P)

        @block.sync
        def _(sp):
            for dst, src in ((id_s, ident), (wq_s, wq_t), (wk_s, wk), (wv_s, wv), (gw_s, gate_t)):
                sp.dma_start(dst[:, :], src).then_inc(s_const, 16)
            for i, src in enumerate((bq, bk, bv)):
                sp.dma_start(b3_s[:, i:i + 1], src).then_inc(s_const, 16)
            for h in range(2):
                sp.dma_start(gb_s[EXPERTS * h:EXPERTS * h + EXPERTS, :], gate_b).then_inc(s_const, 16)
            sp.sem_inc(s_midout, 1)
            sp.sem_inc(s_pickout, 1)
            with sp.Fori(0, BATCH // 2) as pair:
                for h in range(2):
                    hold(sp, s_free, pair * 2 + h + 1, s_gate[0])
                    hold(sp, s_midout, pair * 64 + 32 * h + 1, s_gate[0])
                    for r in (slice(0, P // 2), slice(P // 2, P)):
                        sp.dma_start(tok[r, :, :], tiles(x, pair * 2 + h)[r, :, :]).then_inc(s_x, 16)
                    hold(sp, s_mid, pair * 2 + h + 1, s_gate[0])
                    for r in (slice(0, P // 2), slice(P // 2, P)):
                        sp.dma_start(tiles(mid, pair * 2 + h)[r, :, :], tok[r, :, :]).then_inc(s_midout, 16)
                hold(sp, s_pick, pair + 1, s_gate[0])
                sp.dma_start(picks[:, bass.ds(pair, 1), :].rearrange("p o n -> p (o n)"), logit[:, :]).then_inc(s_pickout, 16)
                hold(sp, s_pickout, pair * 16 + 17, s_gate[0])
            sp.wait_ge(s_midout, 32 * BATCH + 1)
            sp.wait_ge(s_pooled, BATCH)

        @block.tensor
        def _(pe):
            pe.wait_ge(s_const, 10 * 16)
            pe.wait_ge(s_ones, 1)
            with pe.Fori(0, BATCH // 2) as pair:
                hold(pe, s_act, pair * NA + 1, s_gate[1])
                hold(pe, s_v, pair * ND + 1, s_gate[1])
                for n, (kind, h, g, _) in enumerate(jobs):
                    bank = ps[n % NB]
                    if n >= NB:
                        a, d = taken(n - NB)
                        if jobs[n - NB][3] == "act":
                            hold(pe, s_act, pair * NA + a + 1, s_gate[1])
                        else:
                            hold(pe, s_v, pair * ND + d + 1, s_gate[1])
                    if g == 0:
                        a, d = taken(n - 1) if n else (0, 0)
                        if kind in ("u", "u2"):
                            hold(pe, s_unit, pair * 4 + 2 * h + (kind == "u2") + 1, s_gate[1])
                        if kind in ("k", "log"):
                            hold(pe, s_act, pair * NA + a + 1, s_gate[1])
                        if kind == "o":
                            hold(pe, s_diag, pair * 2 + h + 1, s_gate[1])
                            pe.matmul(ps_s[:, 0:P], wq_s[:, :], diag[:, :], start=True, stop=True)
                            pe.matmul(ps_s[0:1, P:2 * P], bkv[:, :], id_s[:, :], start=True, stop=True).then_inc(s_scaled, 1)
                            hold(pe, s_wkv, pair * 4 + 2 * h + 2, s_gate[1])
                        if kind == "pt":
                            hold(pe, s_pick, pair + 1, s_gate[1])
                    if kind in ("u", "u2"):
                        for t in range(4):
                            last = pe.transpose(bank[:, t * P:t * P + P], unit[:, h, 4 * g + t, :], id_s[:, :])
                    if kind in ("k", "v"):
                        w = wk_s if kind == "k" else wv_s
                        last = pe.matmul(bank[:, :], w[:, :], chan[:, g * 512:g * 512 + 512], start=True, stop=True)
                    if kind == "o":
                        for t in range(4):
                            i = 4 * g + t
                            pe.matmul(bank[:, t * P:t * P + P], chan[:, i * P:i * P + P], wkv[:, :], start=True, stop=False)
                            last = pe.matmul(bank[:, t * P:t * P + P], ones[:, :], brow[:, :], start=False, stop=True)
                    if kind == "log":
                        e = slice(EXPERTS * h, EXPERTS * h + EXPERTS)
                        last = pe.matmul(bank[e, :], gw_s[:, :], chan[:, g * 512:g * 512 + 512], start=True, stop=True)
                    if kind == "pt":
                        for t in range(4):
                            i = 4 * g + t
                            last = pe.transpose(bank[:, t * P:t * P + P], logit[:, i * P:i * P + P], id_s[:, :])
                    last.then_inc(s_job, 1)
                hold(pe, s_act, pair * NA + NA + 1, s_gate[1])
                for h in range(2):
                    for t in range(NT):
                        mm = pe.matmul(ps_s[:, 256 + 64 * h:320 + 64 * h], unit[:, h, t, :], k_c[:, t * P + 64 * h:t * P + 64 * h + 64],
                                       start=t == 0, stop=t == NT - 1)
                    mm.then_inc(s_pool, 1)

        @block.scalar
        def _(act):
            act.sem_inc(s_act, 1)
            act.wait_ge(s_const, 10 * 16)
            with act.Fori(0, BATCH // 2) as pair:
                gate = s_gate[2]
                for n, (kind, h, g, who) in enumerate(jobs):
                    if g == 0 and kind in ("u", "u2"):
                        k = pair * 4 + 2 * h + (kind == "u2")
                        hold(act, s_var, k + 1, gate)
                        act.activation(lrt[:, :], lve[:, :], ACT.Sqrt).then_inc(s_std, 1)
                    if kind == "pt" and g == 0:
                        hold(act, s_peak, pair + 1, gate)
                        act.activation(logit[:, :], logit[:, :], ACT.Exp, bias=peak[:, :], accum_out=total[:, :]).then_inc(s_exp, 1)
                    if who != "act":
                        continue
                    hold(act, s_job, pair * NJ + n + 1, gate)
                    bank = ps[n % NB]
                    cols = slice(g * 512, g * 512 + 512)
                    if kind in ("u", "u2"):
                        ins = act.activation(chan[:, cols], bank[:, :], ACT.Copy)
                    if kind == "k":
                        ins = act.activation(k_c[:, cols], bank[:, :], ACT.Identity, bias=b3_s[:, 1:2])
                    if kind == "log":
                        e = slice(EXPERTS * h, EXPERTS * h + EXPERTS)
                        if h == 0 and g == 0:
                            hold(act, s_pickout, pair * 16 + 1, gate)
                        ins = act.activation(logit[e, cols], bank[e, :], ACT.Identity, bias=gb_s[e, :])
                    if kind == "pt":
                        ins = act.activation(k_c[:, cols], bank[:, :], ACT.Copy)
                    ins.then_inc(s_act, 1)

        @block.vector
        def _(dve):
            dve.memset(ones[:, :], 1.0).then_inc(s_ones, 1)
            dve.sem_inc(s_v, 1)
            dve.sem_inc(s_free, 1)
            dve.wait_ge(s_const, 10 * 16)
            with dve.Fori(0, BATCH // 2) as pair:
                gate = s_gate[3]
                step = Chain(dve, s_dve, gate, pair * DVE_STEPS)
                for h in range(2):
                    first = 6 * NG * h
                    b = pair * 2 + h
                    hold(dve, s_x, b * 32 + 32, gate)
                    if h == 0:
                        hold(dve, s_v, pair * ND + 1, gate)
                    token_norm(dve, step, gate, tok, unit[:, h, :, :], lst, lmv, lve[:, :], lrt[:, :], lsc[:, :], 1e-5,
                               s_var, s_std, 2 * b + 1)
                    dve.sem_inc(s_unit, 1)
                    for g in range(NG):
                        n = first + 2 * NG + g
                        hold(dve, s_act, pair * NA + taken(n)[0] + 1, gate)
                        hold(dve, s_job, pair * NJ + n + 1, gate)
                        step(dve.scalar_tensor_tensor(scr[:, :], ps[n % NB][:, :], b3_s[:, 2:3], k_c[:, g * 512:g * 512 + 512],
                                                      ALU.add, ALU.mult, accum_out=part[:, g:g + 1]))
                        dve.sem_inc(s_v, 1)
                    step(dve.tensor_reduce(kv[:, :], part[:, :], AX, ALU.add))
                    step(dve.tensor_scalar(diag[:, :], id_s[:, :], kv[:, :], None, ALU.mult))
                    step(dve.tensor_tensor(bkv[:, :], kv[:, :], b3_s[:, 0:1], ALU.mult))
                    dve.sem_inc(s_diag, 1)
                    hold(dve, s_scaled, b + 1, gate)
                    dve.tensor_copy(wkv[:, :], ps_s[:, 0:P]).then_inc(s_wkv, 1)
                    dve.tensor_copy(brow[:, :], ps_s[0:1, P:2 * P]).then_inc(s_wkv, 1)
                    for g in range(NG):
                        n = first + 3 * NG + g
                        hold(dve, s_job, pair * NJ + n + 1, gate)
                        t4 = tok[:, 4 * g:4 * g + 4, :].rearrange("p t c -> p (t c)")
                        step(dve.tensor_tensor(t4, t4, ps[n % NB][:, :], ALU.add))
                        dve.sem_inc(s_v, 1)
                    dve.sem_inc(s_mid, 1)
                    token_norm(dve, step, gate, tok, unit[:, h, :, :], lst, lmv, lve[:, :], lrt[:, :], lsc[:, :], 1e-5,
                               s_var, s_std, 2 * b + 2)
                    dve.sem_inc(s_unit, 1)
                    dve.sem_inc(s_free, 1)
                n = 12 * NG
                hold(dve, s_act, pair * NA + taken(n - 1)[0] + 1, gate)
                step(dve.tensor_reduce(peak[:, :], logit[:, :], AX, ALU.max))
                step(dve.tensor_scalar(peak[:, :], peak[:, :], -1.0, None, ALU.mult))
                dve.sem_inc(s_peak, 1)
                hold(dve, s_exp, pair + 1, gate)
                step(dve.max(top[:, :], logit[:, :]))
                step(dve.match_replace(rest[:, :], top[:, :], logit[:, :], 0.0))
                step(dve.reciprocal(total[:, :], total[:, :]))
                step(dve.tensor_tensor(logit[:, :], logit[:, :], rest[:, :], ALU.subtract))
                step(dve.tensor_scalar(logit[:, :], logit[:, :], total[:, :], None, ALU.mult))
                dve.sem_inc(s_pick, 1)
                for h in range(2):
                    hold(dve, s_pool, pair * 2 + 2, gate)
                    step(dve.tensor_copy(pooled[:, bass.ds(pair * 2 + h, 1), :].rearrange("p o e -> p (o e)"),
                                         ps_s[:, 256 + 64 * h:320 + 64 * h]))
                    dve.sem_inc(s_pooled, 1)
                assert step.n == DVE_STEPS, step.n


def expert_layer(nc, mid, picks, pooled, w1, b1, w2, b2, ident, out):
    with ExitStack() as ctx:
        st = Stage(nc, ctx, "l2b")
        NE = EXPERTS // EB
        w1_s = [st.sb(f"w1{i}", [P, EB, HIDDEN]) for i in range(2)]
        w2_s = [st.sb(f"w2{i}", [P, EB, HCH, C]) for i in range(2)]
        b1_s = st.sb("b1", [P, EXPERTS, HCH])
        b2_s = st.sb("b2", [P, EXPERTS])
        hid = st.sb("hid", [P, EB, HCH, BATCH])
        act_h = st.sb("act_h", [P, EB, HCH, BATCH])
        res_t = st.sb("res_t", [P, BATCH, EXPERTS])
        res = st.sb("res", [P, BATCH, C])
        pick = st.sb("pick", [P, N])
        tok = st.sb("tok", [P, NT, C])
        id_s = st.sb("id", [P, P])
        ps_h = st.psum("psh", [P, 512])
        ps_o = st.psum("pso", [P, 512])
        ps_r = st.psum("psr", [P, 512])
        ps = [st.psum(f"ps{i}", [P, 512]) for i in range(4)]
        s_const = st.sem("const")
        s_zero = st.sem("zero")
        s_w = [st.sem(f"w{i}") for i in range(2)]
        s_used = st.sem("used")
        s_h = st.sem("h")
        s_hb = st.sem("hb")
        s_gelu = st.sem("gelu")
        s_o = st.sem("o")
        s_ob = st.sem("ob")
        s_tr = st.sem("tr")
        s_res = st.sem("res")
        s_in = st.sem("in")
        s_pk = st.sem("pk")
        s_job = st.sem("job")
        s_add = st.sem("add")
        s_out = st.sem("out")
        s_gate = st.gates()
        block = ctx.enter_context(nc.Block())

        def tiles(dram, b):
            return dram[bass.ds(b, 1), :, :].rearrange("o (t p) c -> (o p) t c", p=P)

        @block.sync
        def _(sp):
            sp.dma_start(id_s[:, :], ident).then_inc(s_const, 16)
            sp.dma_start(b1_s[:, :, :], b1).then_inc(s_const, 16)
            sp.dma_start(b2_s[:, :], b2).then_inc(s_const, 16)
            sp.sem_inc(s_used, 2)
            with sp.Fori(0, NE // 2) as i:
                for s in range(2):
                    e = (2 * i + s) * EB
                    hold(sp, s_used, 2 * i + s + 1, s_gate[0])
                    sp.dma_start(w1_s[s][:, :, :], w1[bass.ds(e, EB), 0:C, :].rearrange("e d h -> d e h")).then_inc(s_w[s], 16)
                    sp.dma_start(w2_s[s][:, :, :, :].rearrange("p e k o -> p e (k o)"),
                                 w2[bass.ds(e, EB), 0:HIDDEN, :].rearrange("e (p k) o -> p e (k o)", k=HCH)).then_inc(s_w[s], 16)
            sp.sem_inc(s_out, 1)
            with sp.Fori(0, BATCH // 2) as pair:
                hold(sp, s_add, pair * 2 * NG + 1, s_gate[0])
                sp.dma_start(pick[:, :], picks[:, bass.ds(pair, 1), :].rearrange("p o n -> p (o n)")).then_inc(s_pk, 16)
                for h in range(2):
                    b = 2 * pair + h
                    hold(sp, s_out, b * 32 + 1, s_gate[0])
                    for r in (slice(0, P // 2), slice(P // 2, P)):
                        sp.dma_start(tok[r, :, :], tiles(mid, b)[r, :, :]).then_inc(s_in, 16)
                    hold(sp, s_add, b * NG + NG + 1, s_gate[0])
                    for r in (slice(0, P // 2), slice(P // 2, P)):
                        sp.dma_start(tiles(out, b)[r, :, :], tok[r, :, :]).then_inc(s_out, 16)
            sp.wait_ge(s_out, 32 * BATCH + 1)

        @block.tensor
        def _(pe):
            pe.wait_ge(s_const, 48)
            with pe.Fori(0, NE // 2) as i:
                for s in range(2):
                    j = 2 * i + s
                    hold(pe, s_w[s], 32 * i + 32, s_gate[1])
                    for e in range(EB):
                        for k in range(HCH):
                            mm = pe.matmul(ps_h[:, (e * HCH + k) * BATCH:(e * HCH + k + 1) * BATCH], w1_s[s][:, e, k:HIDDEN:HCH],
                                           pooled[:, :, bass.ds(j * EB + e, 1)].rearrange("p b o -> p (b o)"), start=True, stop=True)
                    mm.then_inc(s_h, 1)
                    hold(pe, s_gelu, j + 1, s_gate[1])
                    for e in range(EB):
                        for k in range(HCH):
                            mm = pe.matmul(ps_o[:, e * BATCH:(e + 1) * BATCH], w2_s[s][:, e, k, :], act_h[:, e, k, :],
                                           start=k == 0, stop=k == HCH - 1)
                    mm.then_inc(s_o, 1)
                    hold(pe, s_ob, j + 1, s_gate[1])
            for pair in range(BATCH // 2):
                mm = pe.transpose(ps_r[:, pair * C:pair * C + C], res_t[:, 2 * pair:2 * pair + 2, :].rearrange("p b e -> p (b e)"),
                                  id_s[:, :])
            mm.then_inc(s_tr, 1)
            pe.wait_ge(s_res, BATCH)
            with pe.Fori(0, BATCH // 2) as pair:
                hold(pe, s_pk, 16 * pair + 16, s_gate[1])
                for h in range(2):
                    for g in range(NG):
                        n = h * NG + g
                        hold(pe, s_add, pair * 2 * NG + max(0, n - 3) + 1, s_gate[1])
                        for t in range(4):
                            i = 4 * g + t
                            mm = pe.matmul(ps[n % 4][:, t * P:t * P + P], pick[:, i * P:i * P + P],
                                           res[:, bass.ds(2 * pair + h, 1), :].rearrange("p o c -> p (o c)"), start=True, stop=True)
                        mm.then_inc(s_job, 1)

        @block.scalar
        def _(act):
            with act.Fori(0, NE) as j:
                hold(act, s_hb, j + 1, s_gate[2])
                act.activation(act_h[:, :, :, :], hid[:, :, :, :], ACT.Gelu).then_inc(s_gelu, 1)

        @block.vector
        def _(dve):
            dve.memset(res[:, :, :], 0.0).then_inc(s_zero, 1)
            dve.wait_ge(s_const, 48)
            dve.sem_inc(s_add, 1)
            with dve.Fori(0, NE) as j:
                hold(dve, s_h, j + 1, s_gate[3])
                dve.tensor_tensor(hid[:, :, :, :], ps_h[:, 0:EB * HCH * BATCH].rearrange("p (e k b) -> p e k b", k=HCH, b=BATCH),
                                  b1_s[:, bass.ds(j * EB, EB), :].unsqueeze(3).broadcast_to([P, EB, HCH, BATCH]),
                                  ALU.add).then_inc(s_hb, 1)
                hold(dve, s_o, j + 1, s_gate[3])
                dve.tensor_tensor(res_t[:, :, bass.ds(j * EB, EB)], ps_o[:, 0:EB * BATCH].rearrange("p (e b) -> p b e", b=BATCH),
                                  b2_s[:, bass.ds(j * EB, EB)].unsqueeze(1).broadcast_to([P, BATCH, EB]), ALU.add).then_inc(s_ob, 1)
                dve.sem_inc(s_used, 1)
            dve.wait_ge(s_tr, 1)
            dve.wait_ge(s_zero, 1)
            for b in range(BATCH):
                r = slice(EXPERTS * (b % 2), EXPERTS * (b % 2) + EXPERTS)
                dve.tensor_copy(res[r, b, :], ps_r[r, (b // 2) * C:(b // 2) * C + C]).then_inc(s_res, 1)
            with dve.Fori(0, BATCH // 2) as pair:
                for h in range(2):
                    hold(dve, s_in, (2 * pair + h) * 32 + 32, s_gate[3])
                    for g in range(NG):
                        n = h * NG + g
                        hold(dve, s_job, pair * 2 * NG + n + 1, s_gate[3])
                        t4 = tok[:, 4 * g:4 * g + 4, :].rearrange("p t c -> p (t c)")
                        dve.tensor_tensor(t4, t4, ps[n % 4][:, :], ALU.add).then_inc(s_add, 1)


def choose_candidate(nc, log_weights, gumbel, sigma, m_plus, m_minus, m_u, tile_in, chunk_in, mats, mats_u, tile_mask, chunk_mask):
    with ExitStack() as ctx:
        st = Stage(nc, ctx, "l3c")
        z = st.sb("z", [P, SIZES])
        gu = st.sb("gu", [P, SIZES])
        soft = st.sb("soft", [P, SIZES])
        hard = st.sb("hard", [P, SIZES])
        wgt = st.sb("wgt", [P, SIZES])
        none = st.sb("none", [P, 1])
        peak = st.sb("peak", [P, 1])
        total = st.sb("total", [P, 1])
        sg = st.sb("sg", [P, FILTERS])
        mp = st.sb("mp", [P, 2, SIZES, FILTERS, C])
        mu = st.sb("mu", [P, SIZES, LAGS, C])
        tin = st.sb("tin", [P, SIZES, NT])
        cin = st.sb("cin", [CH, SIZES])
        s_in = st.sem("in")
        s_mat = st.sem("mat")
        s_z = st.sem("z")
        s_exp = st.sem("exp")
        s_root = st.sem("root")
        s_dve = st.sem("dve")
        s_end = st.sem("end")
        gate = st.gates()[0]
        block = ctx.enter_context(nc.Block())

        @block.sync
        def _(sp):
            for dst, src in ((z, bcast(log_weights, P)), (gu, bcast(gumbel, P)), (sg, bcast(sigma, P)), (cin, chunk_in)):
                sp.dma_start(dst[:, :], src).then_inc(s_in, 16)
            sp.dma_start(tin[:, :, :], tile_in).then_inc(s_in, 16)
            for i in range(SIZES):
                sp.dma_start(mu[:, i, :, :], m_u[i].rearrange("k d e -> d k e")).then_inc(s_mat, 16)
                for s, m in enumerate((m_plus, m_minus)):
                    sp.dma_start(mp[:, s, i, :, :], m[i].rearrange("k d e -> d k e")).then_inc(s_mat, 16)
            sp.wait_ge(s_end, 1)

        @block.scalar
        def _(act):
            act.wait_ge(s_z, 1)
            act.activation(soft[:, :], z[:, :], ACT.Exp, bias=peak[:, :], accum_out=total[:, :]).then_inc(s_exp, 1)
            for _ in range(2):
                act.activation(sg[:, :], sg[:, :], ACT.Sqrt).then_inc(s_root, 1)
                act.wait_ge(s_root, _ + 1)

        @block.vector
        def _(dve):
            step = Chain(dve, s_dve, gate)
            dve.wait_ge(s_in, 5 * 16)
            step(dve.tensor_tensor(z[:, :], z[:, :], gu[:, :], ALU.add))
            step(dve.tensor_reduce(peak[:, :], z[:, :], AX, ALU.max))
            step(dve.tensor_scalar(peak[:, :], peak[:, :], -1.0, None, ALU.mult))
            dve.sem_inc(s_z, 1)
            dve.wait_ge(s_exp, 1)
            step(dve.reciprocal(total[:, :], total[:, :]))
            step(dve.tensor_scalar(soft[:, :], soft[:, :], total[:, :], None, ALU.mult))
            step(dve.tensor_reduce(peak[:, :], soft[:, :], AX, ALU.max))
            step(dve.tensor_scalar(hard[:, :], soft[:, :], peak[:, :], None, ALU.is_ge))
            step(dve.memset(none[:, :], 1.0))
            for i in range(SIZES):
                step(dve.tensor_tensor(hard[:, i:i + 1], hard[:, i:i + 1], none[:, :], ALU.mult))
                step(dve.tensor_tensor(none[:, :], none[:, :], hard[:, i:i + 1], ALU.subtract))
            step(dve.tensor_tensor(wgt[:, :], hard[:, :], soft[:, :], ALU.subtract))
            step(dve.tensor_tensor(wgt[:, :], wgt[:, :], soft[:, :], ALU.add))
            step(dve.tensor_scalar(tile_mask[:, :], tin[:, 0, :], hard[:, 0:1], None, ALU.mult))
            step(dve.tensor_scalar(chunk_mask[:, :], cin[:, 0:1], hard[0:CH, 0:1], None, ALU.mult))
            for i in range(1, SIZES):
                step(dve.scalar_tensor_tensor(tile_mask[:, :], tin[:, i, :], hard[:, i:i + 1], tile_mask[:, :], ALU.mult, ALU.add))
                step(dve.scalar_tensor_tensor(chunk_mask[:, :], cin[:, i:i + 1], hard[0:CH, i:i + 1], chunk_mask[:, :], ALU.mult, ALU.add))
            dve.wait_ge(s_mat, 3 * SIZES * 16)
            for i in range(SIZES):
                for dst, src in ((mats[:, 0, :, :], mp[:, 0, i, :, :]), (mats[:, 1, :, :], mp[:, 1, i, :, :]), (mats_u[:, :, :], mu[:, i, :, :])):
                    if i == 0:
                        step(dve.tensor_scalar(dst, src, wgt[:, 0:1], None, ALU.mult))
                    else:
                        step(dve.scalar_tensor_tensor(dst, src, wgt[:, i:i + 1], dst, ALU.mult, ALU.add))
            dve.wait_ge(s_root, 2)
            for s in range(2):
                step(dve.tensor_tensor(mats[:, s, :, :], mats[:, s, :, :], sg[:, :].unsqueeze(2).broadcast_to([P, FILTERS, C]), ALU.mult))
            dve.sem_inc(s_end, 1)


def causal_attention_layer(nc, x, w_t, b_qk, b_v, causal, ident, reverse, tile_mask, mats_u, resid, rev):
    V1 = C + 1
    with ExitStack() as ctx:
        st = Stage(nc, ctx, "l3a")
        tok = st.sb("tok", [P, NT, C])
        unit = st.sb("unit", [P, NT, C])
        chan = st.sb("chan", [P, 2 + N])
        q_c = st.sb("q_c", [P, N])
        k_c = st.sb("k_c", [P, N])
        k_t = st.sb("k_t", [P, NT, C])
        v_t = st.sb("v_t", [P, NT, V1])
        att = st.sb("att", [P, NT, P])
        state = st.sb("state", [P, NT, V1])
        ratio = st.sb("ratio", [P, NT, V1])
        scr = st.sb("scr", [P, N])
        id_s = st.sb("id", [P, P])
        rv_s = st.sb("rv", [P, P])
        cs_s = st.sb("cs", [P, P])
        w_s = st.sb("w", [P, 3, C])
        bqk = st.sb("bqk", [P, 2])
        bv_s = st.sb("bv", [1, C])
        ones = st.sb("ones", [1, P])
        den = st.sb("den", [P, NT])
        lst = st.sb("lst", [P, NT, 6])
        lmv = st.sb("lmv", [P, NT, 2])
        lve = st.sb("lve", [P, NT])
        lrt = st.sb("lrt", [P, NT])
        lsc = st.sb("lsc", [P, NT])
        ps = [st.psum(f"ps{i}", [P, 512]) for i in range(8)]
        s_const = st.sem("const")
        s_zero = st.sem("zero")
        s_x = st.sem("x")
        s_job = st.sem("job")
        s_act = st.sem("act")
        s_v = st.sem("v")
        s_var = st.sem("var")
        s_std = st.sem("std")
        s_unit = st.sem("unit")
        s_low = st.sem("low")
        s_exp = st.sem("exp")
        s_elu = st.sem("elu")
        s_rev = st.sem("rev")
        s_res = st.sem("res")
        s_out = st.sem("out")
        s_dve = st.sem("dve")
        s_gate = st.gates()
        PB = 3
        jobs = [("u", g, "act") for g in range(NG)] + [("q", g, "act") for g in range(NG)] + [("k", g, "act") for g in range(NG)]
        jobs += [("v", g, "act") for g in range(NG)] + [("kt", g, "act") for g in range(NG)] + [("a", g, "dve") for g in range(NG)]
        jobs += [("s", j, "dve") for j in range(-(-(NT - 1) // PB))] + [("o", j, "act") for j in range(-(-NT // PB))]
        jobs += [("u2", g, "act") for g in range(NG)] + [("ar", g, "dve") for g in range(NG)] + [("rev", g, "act") for g in range(NG)]
        NJ, NB = len(jobs), len(ps)
        NA = sum(j[2] == "act" for j in jobs)
        ND = NJ - NA

        def taken(n):
            return sum(j[2] == "act" for j in jobs[:n + 1]), sum(j[2] == "dve" for j in jobs[:n + 1])

        FIRST = {kind: min(n for n, j in enumerate(jobs) if j[0] == kind) for kind, *_ in jobs}
        LAST = {kind: max(n for n, j in enumerate(jobs) if j[0] == kind) for kind, *_ in jobs}
        DVE_STEPS = 81
        block = ctx.enter_context(nc.Block())

        def tiles(dram, b):
            return dram[bass.ds(b, 1), :, :].rearrange("o (t p) c -> (o p) t c", p=P)

        HALVES = (slice(0, P // 2), slice(P // 2, P))

        @block.sync
        def _(sp):
            for dst, src in ((id_s, ident), (rv_s, reverse), (cs_s, causal), (bqk, b_qk), (bv_s, b_v)):
                sp.dma_start(dst[:, :], src).then_inc(s_const, 16)
            sp.dma_start(w_s[:, :, :], w_t.rearrange("c (f d) -> c f d", d=C)).then_inc(s_const, 16)
            sp.sem_inc(s_out, 1)
            with sp.Fori(0, BATCH) as b:
                hold(sp, s_out, b * 64 + 1, s_gate[0])
                for r in HALVES:
                    sp.dma_start(tok[r, :, :], tiles(x, b)[r, :, :]).then_inc(s_x, 16)
                hold(sp, s_res, b + 1, s_gate[0])
                for r in HALVES:
                    sp.dma_start(tiles(resid, b)[r, :, :], tok[r, :, :]).then_inc(s_out, 16)
                hold(sp, s_act, b * NA + NA + 1, s_gate[0])
                for r in HALVES:
                    sp.dma_start(tiles(rev, b)[r, :, :], scr[r, :].rearrange("p (t c) -> p t c", c=C)).then_inc(s_out, 16)
            sp.wait_ge(s_out, BATCH * 64 + 1)

        @block.tensor
        def _(pe):
            pe.wait_ge(s_const, 6 * 16)
            pe.wait_ge(s_zero, 4)
            with pe.Fori(0, BATCH) as b:
                gate = s_gate[1]
                hold(pe, s_act, b * NA + 1, gate)
                for n, (kind, g, _) in enumerate(jobs):
                    bank = ps[n % NB]
                    if n >= NB:
                        a, d = taken(n - NB)
                        if jobs[n - NB][2] == "act":
                            hold(pe, s_act, b * NA + a + 1, gate)
                        else:
                            hold(pe, s_v, b * ND + d, gate)
                    if g == 0:
                        a, d = taken(n - 1) if n else (0, 0)
                        if kind == "u":
                            hold(pe, s_unit, b * 2 + 1, gate)
                        if kind == "u2":
                            hold(pe, s_unit, b * 2 + 2, gate)
                        if kind in ("q", "ar"):
                            hold(pe, s_act, b * NA + a + 1, gate)
                        if kind == "kt":
                            hold(pe, s_elu, b * 2 + 2, gate)
                        if kind == "s":
                            hold(pe, s_act, b * NA + taken(LAST["kt"])[0] + 1, gate)
                        if kind == "o":
                            hold(pe, s_v, b * ND + d, gate)
                    if kind in ("u", "u2"):
                        for t in range(4):
                            last = pe.transpose(bank[:, t * P:t * P + P], unit[:, 4 * g + t, :], id_s[:, :])
                    if kind in ("q", "k"):
                        last = pe.matmul(bank[:, :], w_s[:, int(kind == "k"), :], chan[:, 2 + g * 512:2 + g * 512 + 512], start=True, stop=True)
                    if kind == "v":
                        for t in range(4):
                            i = 2 + (4 * g + t) * P
                            pe.matmul(bank[:, t * P:t * P + P], chan[:, i:i + P], w_s[:, 2, :], start=True, stop=False)
                            last = pe.matmul(bank[:, t * P:t * P + P], ones[:, :], bv_s[:, :], start=False, stop=True)
                    if kind == "kt":
                        for t in range(4):
                            i = (4 * g + t) * P
                            last = pe.transpose(bank[:, t * P:t * P + P], k_c[:, i:i + P], id_s[:, :])
                    if kind == "a":
                        for t in range(4):
                            i = (4 * g + t) * P
                            last = pe.matmul(bank[:, t * P:t * P + P], k_c[:, i:i + P], q_c[:, i:i + P], start=True, stop=True)
                    if kind == "s":
                        for t in range(PB * g, min(PB * g + PB, NT - 1)):
                            o = bank[:, (t % PB) * V1:(t % PB) * V1 + V1]
                            last = pe.matmul(o, k_t[:, t, :], v_t[:, t, :], start=True, stop=True)
                    if kind == "o":
                        for t in range(PB * g, min(PB * g + PB, NT)):
                            o = bank[:, (t % PB) * V1:(t % PB) * V1 + V1]
                            pe.matmul(o, att[:, t, :], v_t[:, t, :], start=True, stop=False)
                            last = pe.matmul(o, q_c[:, t * P:t * P + P], state[:, t, :], start=False, stop=True)
                    if kind == "ar":
                        for t in range(4):
                            for lag in range(LAGS):
                                i = 2 + (4 * g + t) * P - lag
                                last = pe.matmul(bank[:, t * P:t * P + P], chan[:, i:i + P], mats_u[:, lag, :],
                                                 start=lag == 0, stop=lag == LAGS - 1)
                    if kind == "rev":
                        last = pe.matmul(bank[:, :], rv_s[:, :], unit[:, 4 * g:4 * g + 4, :].rearrange("p t c -> p (t c)"), start=True, stop=True)
                    last.then_inc(s_job, 1)

        @block.scalar
        def _(act):
            act.sem_inc(s_act, 1)
            act.wait_ge(s_const, 6 * 16)
            with act.Fori(0, BATCH) as b:
                gate = s_gate[2]
                for n, (kind, g, who) in enumerate(jobs):
                    if g == 0 and kind in ("u", "u2"):
                        k = b * 2 + (kind == "u2")
                        hold(act, s_var, k + 1, gate)
                        act.activation(lrt[:, :], lve[:, :], ACT.Sqrt).then_inc(s_std, 1)
                    if g == 0 and kind in ("k", "v"):
                        hold(act, s_low, b * 2 + int(kind == "v") + 1, gate)
                        act.activation(scr[:, :], scr[:, :], ACT.Exp).then_inc(s_exp, 1)
                    if who != "act":
                        continue
                    hold(act, s_job, b * NJ + n + 1, gate)
                    bank = ps[n % NB]
                    cols = slice(g * 512, g * 512 + 512)
                    four = slice(4 * g, 4 * g + 4)
                    if kind in ("u", "u2"):
                        ins = act.activation(chan[:, 2 + g * 512:2 + g * 512 + 512], bank[:, :], ACT.Copy)
                    if kind == "q":
                        ins = act.activation(q_c[:, cols], bank[:, :], ACT.Identity, bias=bqk[:, 0:1])
                    if kind == "k":
                        ins = act.activation(k_c[:, cols], bank[:, :], ACT.Identity, bias=bqk[:, 1:2])
                    if kind == "v":
                        ins = act.activation(v_t[:, four, 0:C], bank[:, :].rearrange("p (t c) -> p t c", c=C), ACT.Copy)
                    if kind == "kt":
                        ins = act.activation(k_t[:, four, :].rearrange("p t c -> p (t c)"), bank[:, :], ACT.Copy)
                    if kind == "o":
                        k = min(PB, NT - PB * g)
                        ins = act.activation(ratio[:, PB * g:PB * g + k, :].rearrange("p t c -> p (t c)"), bank[:, 0:k * V1], ACT.Copy)
                    if kind == "rev":
                        ins = act.activation(scr[:, cols], bank[:, :], ACT.Copy)
                    ins.then_inc(s_act, 1)

        @block.vector
        def _(dve):
            dve.memset(ones[:, :], 1.0).then_inc(s_zero, 1)
            dve.memset(chan[:, 0:2], 0.0).then_inc(s_zero, 1)
            dve.memset(v_t[:, :, C], 1.0).then_inc(s_zero, 1)
            dve.memset(state[:, 0, :], 0.0).then_inc(s_zero, 1)
            dve.wait_ge(s_zero, 4)
            dve.wait_ge(s_const, 6 * 16)
            with dve.Fori(0, BATCH) as b:
                gate = s_gate[3]
                step = Chain(dve, s_dve, gate, b * DVE_STEPS)
                hold(dve, s_x, b * 32 + 32, gate)
                hold(dve, s_act, b * NA + 1, gate)
                token_norm(dve, step, gate, tok, unit, lst, lmv, lve[:, :], lrt[:, :], lsc[:, :], 1e-5, s_var, s_std, 2 * b + 1)
                dve.sem_inc(s_unit, 1)
                hold(dve, s_out, b * 64 + 1, gate)
                for i, (kind, src) in enumerate((("q", q_c), ("k", k_c))):
                    hold(dve, s_act, b * NA + taken(LAST[kind])[0] + 1, gate)
                    step(dve.tensor_scalar(scr[:, :], src[:, :], 0.0, None, ALU.min))
                    dve.sem_inc(s_low, 1)
                    hold(dve, s_exp, 2 * b + i + 1, gate)
                    step(dve.scalar_tensor_tensor(src[:, :], src[:, :], 0.0, scr[:, :], ALU.max, ALU.add))
                    dve.sem_inc(s_elu, 1)
                for n, (kind, g, who) in enumerate(jobs):
                    if kind == "a":
                        hold(dve, s_job, b * NJ + n + 1, gate)
                        step(dve.tensor_tensor(att[:, 4 * g:4 * g + 4, :], ps[n % NB][:, :].rearrange("p (t k) -> p t k", k=P),
                                               cs_s[:, :].unsqueeze(1).broadcast_to([P, 4, P]), ALU.mult))
                        dve.sem_inc(s_v, 1)
                    if kind == "s":
                        hold(dve, s_job, b * NJ + n + 1, gate)
                        for t in range(PB * g, min(PB * g + PB, NT - 1)):
                            o = ps[n % NB][:, (t % PB) * V1:(t % PB) * V1 + V1]
                            step(dve.tensor_tensor(state[:, t + 1, :], state[:, t, :], o, ALU.add))
                        dve.sem_inc(s_v, 1)
                hold(dve, s_act, b * NA + taken(LAST["o"])[0] + 1, gate)
                step(dve.tensor_scalar(den[:, :], ratio[:, :, C], 1e-6, None, ALU.add))
                step(dve.reciprocal(den[:, :], den[:, :]))
                step(dve.tensor_tensor(ratio[:, :, 0:C], ratio[:, :, 0:C], den[:, :].unsqueeze(2).broadcast_to([P, NT, C]), ALU.mult))
                step(dve.tensor_tensor(tok[:, :, :], tok[:, :, :], ratio[:, :, 0:C], ALU.add))
                token_norm(dve, step, gate, tok, unit, lst, lmv, lve[:, :], lrt[:, :], lsc[:, :], 1e-5, s_var, s_std, 2 * b + 2)
                dve.sem_inc(s_unit, 1)
                part = ratio[:, 0:4, 0:C]
                for n, (kind, g, who) in enumerate(jobs):
                    if kind == "ar":
                        hold(dve, s_job, b * NJ + n + 1, gate)
                        four = slice(4 * g, 4 * g + 4)
                        step(dve.tensor_tensor(part, ps[n % NB][:, :].rearrange("p (t c) -> p t c", c=C),
                                               tile_mask[:, four].unsqueeze(2).broadcast_to([P, 4, C]), ALU.mult))
                        dve.sem_inc(s_v, 1)
                        step(dve.tensor_tensor(tok[:, four, :], tok[:, four, :], part, ALU.add))
                dve.sem_inc(s_res, 1)
                assert step.n == DVE_STEPS, step.n


def spectral_transforms(nc, rev, phi, dft_phi, dft_x, phi_hat, x_hat):
    with ExitStack() as ctx:
        st = Stage(nc, ctx, "l3t")
        KC = 4 * DELTA
        ph = st.sb("ph", [CH + 1, FILTERS * DELTA])
        dp = st.sb("dp", [CH + 1, 2, P])
        dx = st.sb("dx", [CH, P])
        hat = st.sb("hat", [P, 2, FILTERS * DELTA])
        xin = [st.sb(f"xin{i}", [CH, CH * C]) for i in range(2)]
        xout = [st.sb(f"xout{i}", [P, CH * C]) for i in range(2)]
        ps = [st.psum(f"ps{i}", [P, 512]) for i in range(8)]
        s_const = st.sem("const")
        s_in = [st.sem(f"in{i}") for i in range(2)]
        s_job = st.sem("job")
        s_act = st.sem("act")
        s_dve = st.sem("dve")
        s_out = st.sem("out")
        s_used = st.sem("used")
        s_store = [st.sem(f"store{i}") for i in range(2)]
        s_gate = st.gates()
        NX = CH * C // 512
        block = ctx.enter_context(nc.Block())

        @block.sync
        def _(sp):
            sp.dma_start(ph[:, :], phi).then_inc(s_const, 16)
            sp.dma_start(dp[:, :, :], dft_phi).then_inc(s_const, 16)
            sp.dma_start(dx[:, :], dft_x).then_inc(s_const, 16)
            sp.sem_inc(s_used, 2)
            with sp.Fori(0, BATCH // 2) as i:
                for s in range(2):
                    b = 2 * i + s
                    hold(sp, s_used, b + 1, s_gate[0])
                    sp.dma_start(xin[s][:, :], rev[bass.ds(b, 1), :, :].rearrange("o (c s) d -> (o c) (s d)", s=CH)).then_inc(s_in[s], 16)
            sp.wait_ge(s_out, 16 * 4)
            for s in range(2):
                sp.wait_ge(s_store[s], 16 * (BATCH // 2) + 1)

        @block.tensor
        def _(pe):
            pe.wait_ge(s_const, 48)
            for ri in range(2):
                for g in range(4):
                    pe.matmul(ps[4 * ri + g][:, 0:KC], dp[:, ri, :], ph[:, g * KC:g * KC + KC], start=True, stop=True).then_inc(s_job, 1)
            with pe.Fori(0, BATCH // 2) as i:
                for s in range(2):
                    b = 2 * i + s
                    hold(pe, s_in[s], 16 * i + 16, s_gate[1])
                    for g in range(NX):
                        hold(pe, s_act if g % 2 == 0 else s_dve, b * (NX // 2) + g // 2 + 1, s_gate[1])
                        pe.matmul(ps[g % 8][:, :], dx[:, :], xin[s][:, g * 512:g * 512 + 512], start=True, stop=True).then_inc(s_job, 1)

        def take(eng, own, store, parity):
            for ri in range(2):
                for g in range(parity, 4, 2):
                    eng.wait_ge(s_job, 4 * ri + g + 1)
                    store(hat[:, ri, g * KC:g * KC + KC], ps[4 * ri + g][:, 0:KC]).then_inc(own, 1)

        def take_image(eng, own, store, parity, gate, i, s):
            b = 2 * i + s
            for g in range(parity, NX, 2):
                hold(eng, s_job, 8 + b * NX + g + 1, gate)
                if g == parity:
                    hold(eng, s_store[s], i * 16 + 1, gate)
                store(xout[s][:, g * 512:g * 512 + 512], ps[g % 8][:, :]).then_inc(own, 1)

        @block.scalar
        def _(act):
            for s in range(2):
                act.sem_inc(s_store[s], 1)
            take(act, s_act, lambda o, i: act.activation(o, i, ACT.Copy), 0)
            act.wait_ge(s_act, 4)
            act.wait_ge(s_dve, 4)
            for ri in range(2):
                for pl in range(2):
                    act.dma_start(phi_hat[ri, :, :, pl, :], hat[CH * pl:CH * pl + CH, ri, :].rearrange("w (k j) -> w k j", j=DELTA)).then_inc(s_out, 16)
            with act.Fori(0, BATCH // 2) as i:
                for s in range(2):
                    b = 2 * i + s
                    take_image(act, s_act, lambda o, q: act.activation(o, q, ACT.Copy), 0, s_gate[2], i, s)
                    hold(act, s_act, b * (NX // 2) + NX // 2 + 4, s_gate[2])
                    hold(act, s_dve, b * (NX // 2) + NX // 2 + 4, s_gate[2])
                    act.sem_inc(s_used, 1)
                    act.dma_start(x_hat[bass.ds(b, 1), :, :].rearrange("o w n -> (o w) n"), xout[s][:, :]).then_inc(s_store[s], 16)

        @block.vector
        def _(dve):
            take(dve, s_dve, lambda o, i: dve.tensor_copy(o, i), 1)
            with dve.Fori(0, BATCH // 2) as i:
                for s in range(2):
                    take_image(dve, s_dve, lambda o, q: dve.tensor_copy(o, q), 1, s_gate[3], i, s)


def spectral_products(nc, x_hat, phi_hat, mats, ident, y_hat):
    KG, KN = 4, FILTERS // 4
    HALF = CH // 2
    with ExitStack() as ctx:
        st = Stage(nc, ctx, "l3p")
        xr = [st.sb(f"xr{i}", [P, BATCH, 2, C]) for i in range(2)]
        fr = [st.sb(f"fr{i}", [P, FILTERS * 2, CH]) for i in range(2)]
        xs = [[st.sb(f"xs{i}{h}", [P, BATCH, 2, C], F32R) for h in range(2)] for i in range(2)]
        fs = [[st.sb(f"fs{i}{q}", [P, 2, FILTERS * 2, HALF], F32R) for q in range(2)] for i in range(2)]
        u = [[st.sb(f"u{i}{h}", [P, KN, 4, BATCH, CH], F32R) for h in range(2)] for i in range(2)]
        mh = st.sb("mh", [P, 2, FILTERS, C], F32R)
        ml = st.sb("ml", [P, 2, FILTERS, C], F32R)
        even = st.sb("even", [P, FILTERS, C])
        yt = [st.sb(f"yt{i}", [P, 512]) for i in range(2)]
        ys = [st.sb(f"ys{i}", [P, BATCH, C]) for i in range(2)]
        id_s = st.sb("id", [P, P])
        ps = [st.psum(f"ps{i}", [P, 512]) for i in range(4)]
        ps_y = [st.psum(f"psy{i}", [P, 512]) for i in range(2)]
        ps_t = [st.psum(f"pst{i}", [P, 512]) for i in range(2)]
        s_const = st.sem("const")
        s_mat = st.sem("mat")
        s_in = [st.sem(f"in{i}") for i in range(2)]
        s_pool = st.sem("pool")
        s_conv = st.sem("conv")
        s_hi = st.sem("hi")
        s_lo = st.sem("lo")
        s_mix = st.sem("mix")
        s_yt = st.sem("yt")
        s_tr = st.sem("tr")
        s_ys = st.sem("ys")
        s_out = [st.sem(f"out{i}") for i in range(2)]
        s_gate = st.gates()
        GJ = 2 * BATCH
        IJ = KG * GJ
        SPLITS = 10
        PAIRS = FREQ // 2
        LOADS = 8 * 16
        block = ctx.enter_context(nc.Block())

        @block.sync
        def _(sp):
            sp.dma_start(id_s[:, :], ident).then_inc(s_const, 16)
            row = FILTERS * 2 * DELTA
            with sp.Fori(0, PAIRS) as i:
                for s in range(2):
                    w = 2 * i + s
                    hold(sp, s_pool, (w + 1) * SPLITS, s_gate[0])
                    for ri in range(2):
                        for copy in range(2):
                            r = slice(CH * copy + HALF * ri, CH * copy + HALF * ri + HALF)
                            sp.dma_start(xr[s][r, :, :, :].rearrange("p b q c -> p b (q c)"),
                                         x_hat[:, ri, bass.ds(w, 1), :, :].rearrange("b o (j q) d -> (o j) b (q d)", q=2)).then_inc(s_in[s], 16)
                        for q in range(2):
                            r = slice(CH * q + HALF * ri, CH * q + HALF * ri + HALF)
                            window = bass.AP(phi_hat.tensor, (ri * FREQ + w) * row + q, [[2, HALF], [DELTA, 2 * FILTERS], [1, CH]])
                            sp.dma_start(fr[s][r, :, :], window).then_inc(s_in[s], 16)

        @block.gpsimd
        def _(pool):
            pool.sem_inc(s_pool, 2 * SPLITS)
            with pool.Fori(0, PAIRS) as i:
                for s in range(2):
                    w = 2 * i + s
                    hold(pool, s_in[s], LOADS * i + LOADS, s_gate[1])
                    hold(pool, s_conv, w * IJ + IJ, s_gate[1])
                    raw = [fr[s][CH * q:CH * q + CH, :, :].rearrange("p k (t a) -> p a k t", a=2) for q in range(2)]
                    hi = [fs[s][q][CH * q:CH * q + CH, :, :, :] for q in range(2)]
                    lo = [fs[s][q][CH - CH * q:P - CH * q, :, :, :] for q in range(2)]
                    step = Chain(pool, s_pool, s_gate[1], (w + 2) * SPLITS)
                    step(pool.tensor_copy(xs[s][0][:, :, :, :], xr[s][:, :, :, :]))
                    for q in range(2):
                        for a in range(2):
                            step(pool.tensor_copy(hi[q][:, a], raw[q][:, a]))
                    step(pool.tensor_tensor(xs[s][1][:, :, :, :], xr[s][:, :, :, :], xs[s][0][:, :, :, :], ALU.subtract))
                    for q in range(2):
                        for a in range(2):
                            step(pool.tensor_tensor(lo[q][:, a], raw[q][:, a], hi[q][:, a], ALU.subtract))
                    assert step.n == SPLITS

        @block.tensor
        def _(pe):
            gate = s_gate[2]
            pe.sem_inc(s_conv, 2 * IJ)
            pe.wait_ge(s_const, 16)
            pe.wait_ge(s_mat, 7)

            def conv(w, s, kg, j):
                q, b = j // BATCH, j % BATCH
                if kg == 0 and j == 0:
                    hold(pe, s_pool, (w + 3) * SPLITS, gate)
                hold(pe, s_lo, w * IJ + kg * GJ + j + 1, gate)
                for part in (1, 0):
                    mm = pe.matmul(ps[j % 4][:, :], xs[s][part][:, b, q, :], fs[s][q][:, :, kg * 2 * KN:(kg + 1) * 2 * KN, :].rearrange("p a k t -> p a (k t)"),
                                   start=part == 1, stop=part == 0)
                mm.then_inc(s_conv, 1)

            def mixes(s, kg):
                todo = [(k, par, m, part) for m, part in ((ml, 0), (mh, 1), (mh, 0)) for par in range(2) for k in range(KN)]
                for n, (k, par, m, part) in enumerate(todo):
                    yield pe.matmul(ps_y[s][:, :], m[:, par, kg * KN + k, :], u[kg % 2][part][:, k, par::2, :, :].rearrange("p x b n -> p x (b n)"),
                                    start=kg == 0 and n == 0, stop=kg == KG - 1 and n == len(todo) - 1)

            def mixed(w, s, kg, following):
                hold(pe, s_lo, w * IJ + (kg + 1) * GJ + 4, gate)
                if kg == 0:
                    hold(pe, s_yt, w + 1, gate)
                todo = mixes(s, kg)
                for j in range(GJ if following else 0):
                    conv(*following, j)
                    for _ in range(2):
                        next(todo)
                for mm in todo:
                    pass
                mm.then_inc(s_mix, 1)

            def transposes(w, s):
                hold(pe, s_yt, w + 3, gate)
                hold(pe, s_ys, w + 1, gate)
                for b in range(BATCH):
                    mm = pe.transpose(ps_t[s][:, b * P:b * P + P], yt[s][:, b * P:b * P + P], id_s[:, :])
                mm.then_inc(s_tr, 1)

            def pair(i, first=False, last=False):
                for s in range(2):
                    w = 2 * i + s
                    for kg in range(KG):
                        if kg + 1 < KG:
                            mixed(w, s, kg, (w, s, kg + 1))
                        else:
                            mixed(w, s, kg, None if last and s == 1 else (w + 1, 1 - s, 0))
                        if kg == 0 and not (first and s == 0):
                            transposes(w - 1, 1 - s)

            for j in range(GJ):
                conv(0, 0, 0, j)
            pair(0, first=True)
            with pe.Fori(1, PAIRS - 1) as i:
                pair(i)
            pair(PAIRS - 1, last=True)
            transposes(FREQ - 1, 1)

        def slots(tile, j):
            q, b = j // BATCH, j % BATCH
            return (tile[:, :, 0::3, b, :] if q == 1 else tile[:, :, 1:3, b, :]).rearrange("p k x n -> p x k n")

        def result(j):
            return ps[j % 4][:, :].rearrange("p (x k n) -> p x k n", x=2, n=CH)

        @block.scalar
        def _(act):
            gate = s_gate[3]
            act.sem_inc(s_yt, 2)

            def sums(w, s):
                hold(act, s_mix, w * KG + KG + 2, gate)
                hold(act, s_tr, w + 1, gate)
                act.activation(yt[s][:, :].rearrange("p (k t a) -> p a k t", a=2, t=HALF), ps_y[s][:, :].rearrange("p (a k t) -> p a k t", a=2, t=HALF),
                               ACT.Copy).then_inc(s_yt, 1)

            def store(w, s):
                hold(act, s_ys, w + 3, gate)
                for ri in range(2):
                    r = slice(CH * ri, CH * ri + CH)
                    at = slice(w, w + 1) if isinstance(w, int) else bass.ds(w, 1)
                    act.dma_start(y_hat[:, ri, at, :, :].rearrange("b o s d -> (o s) b d"), ys[s][r, :, :]).then_inc(s_out[s], 16)

            def pair(i, first=False):
                for s in range(2):
                    w = 2 * i + s
                    for kg in range(KG):
                        hold(act, s_mix, w * KG + kg + 1, gate)
                        for j in range(GJ):
                            hold(act, s_conv, (w + 2) * IJ + kg * GJ + j + 1, gate)
                            act.activation(slots(u[kg % 2][0], j), result(j), ACT.Copy).then_inc(s_hi, 1)
                        if not (first and s == 0):
                            if kg == 0:
                                sums(w - 1, 1 - s)
                            if kg == 2:
                                store(w - 1, 1 - s)

            pair(0, first=True)
            with act.Fori(1, PAIRS) as i:
                pair(i)
            sums(FREQ - 1, 1)
            store(FREQ - 1, 1)

        @block.vector
        def _(dve):
            gate = s_gate[4]
            dve.sem_inc(s_lo, 4)
            dve.sem_inc(s_ys, 2)
            dve.sem_inc(s_mix, 2)
            dve.sem_inc(s_tr, 2)
            dve.sem_inc(s_out[0], 1)
            dve.sem_inc(s_out[1], 1)
            dve.tensor_tensor(mh[:, 0], mats[:, 0], mats[:, 1], ALU.add).then_inc(s_mat, 1)
            dve.tensor_tensor(mh[:, 1], mats[:, 0], mats[:, 1], ALU.subtract).then_inc(s_mat, 1)
            dve.wait_ge(s_mat, 2)
            dve.tensor_tensor(even[:, :, :], mats[:, 0], mats[:, 1], ALU.add).then_inc(s_mat, 1)
            dve.wait_ge(s_mat, 3)
            dve.tensor_tensor(mats[:, 1], mats[:, 0], mats[:, 1], ALU.subtract).then_inc(s_mat, 1)
            dve.wait_ge(s_mat, 4)
            dve.tensor_tensor(ml[:, 0], even[:, :, :], mh[:, 0].bitcast(F32), ALU.subtract).then_inc(s_mat, 1)
            dve.tensor_tensor(ml[:, 1], mats[:, 1], mh[:, 1].bitcast(F32), ALU.subtract).then_inc(s_mat, 1)
            dve.wait_ge(s_mat, 6)
            dve.sem_inc(s_mat, 1)

            def copy_out(w, s, stored):
                hold(dve, s_tr, w + 3, gate)
                hold(dve, s_out[s], stored, gate)
                dve.tensor_copy(ys[s][:, :, :].rearrange("p b c -> p (b c)"), ps_t[s][:, :]).then_inc(s_ys, 1)

            def pair(i, first=False):
                for s in range(2):
                    w = 2 * i + s
                    for kg in range(KG):
                        for j in range(GJ):
                            hold(dve, s_hi, w * IJ + kg * GJ + j + 1, gate)
                            dve.tensor_tensor(slots(u[kg % 2][1], j), result(j), slots(u[kg % 2][0], j), ALU.subtract).then_inc(s_lo, 1)
                        if kg == 1 and not (first and s == 0):
                            copy_out(w - 1, 1 - s, 32 * (i - 1 + s) + 1)

            pair(0, first=True)
            with dve.Fori(1, PAIRS) as i:
                pair(i)
            copy_out(FREQ - 1, 1, 32 * (PAIRS - 1) + 1)
            for s in range(2):
                dve.wait_ge(s_out[s], 32 * PAIRS + 1)


def spectral_return(nc, y_hat, dft_y, chunk_mask, resid, out):
    with ExitStack() as ctx:
        st = Stage(nc, ctx, "l3r")
        yin = [st.sb(f"yin{i}", [P, CH * C]) for i in range(2)]
        tok = [st.sb(f"tok{i}", [CH, CH * C]) for i in range(2)]
        dy = st.sb("dy", [P, CH])
        ps = [st.psum(f"ps{i}", [P, 512]) for i in range(4)]
        s_const = st.sem("const")
        s_in = [st.sem(f"in{i}") for i in range(2)]
        s_job = st.sem("job")
        s_add = st.sem("add")
        s_out = [st.sem(f"out{i}") for i in range(2)]
        s_gate = st.gates()
        NX = CH * C // 512
        block = ctx.enter_context(nc.Block())

        def chunks(dram, b):
            return dram[bass.ds(b, 1), :, :].rearrange("o (c s) d -> (o c) (s d)", s=CH)

        @block.sync
        def _(sp):
            sp.dma_start(dy[:, :], dft_y).then_inc(s_const, 16)
            for s in range(2):
                sp.sem_inc(s_out[s], 1)
            with sp.Fori(0, BATCH // 2) as i:
                for s in range(2):
                    b = 2 * i + s
                    hold(sp, s_out[s], 16 * i + 1, s_gate[0])
                    sp.dma_start(yin[s][:, :], y_hat[bass.ds(b, 1), :, :, :, :].rearrange("b a w s d -> (b a w) (s d)")).then_inc(s_in[s], 16)
                    sp.dma_start(tok[s][:, :], chunks(resid, b)).then_inc(s_in[s], 16)

        @block.tensor
        def _(pe):
            pe.wait_ge(s_const, 16)
            with pe.Fori(0, BATCH // 2) as i:
                for s in range(2):
                    hold(pe, s_in[s], 32 * i + 32, s_gate[1])
                    for g in range(NX):
                        hold(pe, s_add, (2 * i + s) * NX + g + 1, s_gate[1])
                        pe.matmul(ps[g % 4][0:CH, :], dy[:, :], yin[s][:, g * 512:g * 512 + 512], start=True, stop=True).then_inc(s_job, 1)

        @block.vector
        def _(dve):
            dve.sem_inc(s_add, 4)
            with dve.Fori(0, BATCH // 2) as i:
                for s in range(2):
                    for g in range(NX):
                        hold(dve, s_job, (2 * i + s) * NX + g + 1, s_gate[2])
                        t = tok[s][:, g * 512:g * 512 + 512]
                        dve.scalar_tensor_tensor(t, ps[g % 4][0:CH, :], chunk_mask[:, :], t, ALU.mult, ALU.add).then_inc(s_add, 1)

        @block.scalar
        def _(act):
            with act.Fori(0, BATCH // 2) as i:
                for s in range(2):
                    b = 2 * i + s
                    hold(act, s_add, (b + 1) * NX + 4, s_gate[3])
                    act.dma_start(chunks(out, b), tok[s][:, :]).then_inc(s_out[s], 16)
            for s in range(2):
                act.wait_ge(s_out[s], 16 * (BATCH // 2) + 1)


def host_constants():
    p = np.arange(P)
    ident = np.eye(P, dtype=np.float32)
    gmean = (p[:, None] // 4 == p[None, :] // 4).astype(np.float32) / 4
    k = np.arange(TAPS)
    dil = 2 * np.arange(GROUPS) + 1
    by = ((k // 3 - 1)[None, :] * dil[:, None]).reshape(-1)
    bx = ((k % 3 - 1)[None, :] * dil[:, None]).reshape(-1)
    cy = ((p // W)[:, None] + by[None, :]).astype(np.float32)
    ctile = np.broadcast_to(2 * np.arange(NT), (P, NT)).astype(np.float32)
    cx = ((p % W)[:, None] + bx[None, :]).astype(np.float32)
    base = np.broadcast_to(TH + 1 + np.repeat(np.arange(GROUPS), TAPS) * TH * TH, (P, GT)).astype(np.float32)
    w = np.arange(FREQ)
    c65 = np.arange(CH + 1)
    turn = 2 * np.pi * np.outer(c65, w) / (2 * FREQ)
    cos, sin, alt = np.cos(turn), np.sin(turn), (-1.0) ** c65
    zero, one = np.zeros(CH + 1), np.ones(CH + 1)

    def item0(m, col):
        m = m.copy()
        m[:, 0] = col
        return m

    dft_phi = np.stack([np.concatenate([item0(cos, one), item0(-sin, zero)], 1), np.concatenate([item0(sin, zero), item0(cos, alt)], 1)], 1)
    dft_x = np.concatenate([item0(cos, one), item0(-sin, alt)], 1)[:CH]
    dft_y = np.concatenate([item0(2 * cos, one), item0(-2 * sin, alt)], 1)[:CH].T / (2 * FREQ)
    s = p % CH
    reverse = (p[:, None] // CH == p[None, :] // CH) & (s[:, None] + s[None, :] == CH - 1)
    causal = p[:, None] <= p[None, :]
    tile_in = np.broadcast_to(np.arange(NT)[None, :] < (NT >> np.arange(SIZES))[:, None], (P, SIZES, NT))
    chunk_in = np.arange(CH)[:, None] < (CH >> np.arange(SIZES))[None, :]
    l3 = dict(dft_phi=dft_phi, dft_x=dft_x, dft_y=dft_y, reverse=reverse, causal=causal, tile_in=tile_in, chunk_in=chunk_in)
    l3 = {n: a.astype(np.float32) for n, a in l3.items()}
    return dict(**l3, ident=ident, gmean=gmean, cy=cy, cx=cx, ctile=ctile, base=base)




def l0_arrays(i):
    a = {n: np.asarray(i["L0_conv_" + n]) for n in ("w_qkv", "b_qkv", "w_dw", "b_dw", "pconv_off_w", "w_off", "b_off", "pconv_mask_w", "w_mask", "b_mask", "w_proj", "b_proj")}
    return dict(
        l0_w_qkv=a["w_qkv"], l0_b_qkv=a["b_qkv"].reshape(3, P).T, l0_w_dw=a["w_dw"].reshape(3 * C, TAPS), l0_b_dw=a["b_dw"].reshape(3, P).T,
        l0_pconv_off=a["pconv_off_w"].transpose(4, 2, 3, 0, 1).reshape(3 * HC, 3, GROUPS * HC),
        l0_pconv_mask=a["pconv_mask_w"].transpose(3, 1, 2, 0).reshape(3 * HC, 3, HC),
        l0_w_off=a["w_off"].transpose(2, 0, 1), l0_b_off=a["b_off"].reshape(-1),
        l0_w_mask=a["w_mask"].T, l0_b_mask=a["b_mask"], l0_w_proj=a["w_proj"], l0_b_proj=a["b_proj"].reshape(1, C))


def layer0(nc, x, out, A):
    records = nc.dram_tensor("records", (BATCH, GROUPS, TH, TH, CORNERS, 2 * HC), F32).ap()
    meta = nc.dram_tensor("meta", (BATCH, NT, P, META), F32).ap()
    project_and_sample_points(nc, x, A["l0_w_qkv"], A["l0_b_qkv"], A["l0_w_dw"], A["l0_b_dw"], A["l0_pconv_off"], A["l0_pconv_mask"],
                              A["l0_w_off"], A["l0_b_off"], A["l0_w_mask"], A["l0_b_mask"], A["ident"], A["gmean"], A["cy"], A["cx"], A["ctile"],
                              A["base"], records, meta)
    sample_and_attend(nc, x.rearrange("b (t p) c -> (b t) p c", p=P), records.rearrange("b g y x c d -> (b g y x) (c d)"),
                      meta.rearrange("b t p m -> (b t) p m"), A["l0_w_proj"], A["l0_b_proj"], A["ident"],
                      out.rearrange("b (t p) c -> (b t) p c", p=P))


def l1_arrays(i):
    return dict(l1_w_qkv=i["L1_conv_w_qkv"], l1_w_out=i["L1_conv_w_out"], l1_b_out=np.asarray(i["L1_conv_b_out"]).reshape(1, C),
                l1_ln_scale=i["L1_conv_ln_scale"])


def layer1(nc, x, out, A):
    linear_attention_layer(nc, x, A["l1_w_qkv"], A["l1_w_out"], A["l1_b_out"], A["l1_ln_scale"], A["ident"], A["gmean"], out)


def l2_arrays(i):
    a = {n: np.asarray(i["L2_" + n]) for n in ("attn_Wq", "attn_bq", "attn_Wk", "attn_bk", "attn_Wv", "attn_bv", "ffn_gate_w",
                                               "ffn_gate_b", "ffn_weight1", "ffn_weight2")}
    return dict(
        l2_wq_t=a["attn_Wq"].T, l2_wk=a["attn_Wk"], l2_wv=a["attn_Wv"], l2_bq=a["attn_bq"].reshape(C, 1),
        l2_bk=a["attn_bk"].reshape(C, 1), l2_bv=a["attn_bv"].reshape(C, 1), l2_gate_t=a["ffn_gate_w"].T,
        l2_gate_b=a["ffn_gate_b"].reshape(-1, 1), l2_w1=a["ffn_weight1"], l2_w2=a["ffn_weight2"],
        l2_b1=a["ffn_weight1"][:, C, :].reshape(EXPERTS, P, HCH).transpose(1, 0, 2), l2_b2=a["ffn_weight2"][:, HIDDEN, :].T)


def layer2(nc, x, out, A):
    mid = nc.dram_tensor("l2_mid", (BATCH, N, C), F32).ap()
    picks = nc.dram_tensor("l2_picks", (P, BATCH // 2, N), F32).ap()
    with nc.sbuf_tensor("l2_pooled", [P, BATCH, EXPERTS], F32) as pooled:
        gate_layer(nc, x, A["l2_wq_t"], A["l2_wk"], A["l2_wv"], A["l2_bq"], A["l2_bk"], A["l2_bv"], A["l2_gate_t"], A["l2_gate_b"],
                   A["ident"], mid, picks, pooled)
        expert_layer(nc, mid, picks, pooled, A["l2_w1"], A["l2_b1"], A["l2_w2"], A["l2_b2"], A["ident"], out)


def l3_arrays(i):
    a = {n: np.asarray(i["L3_" + n]) for n in ("attn_W", "attn_b", "ffn_sigma", "ffn_phi", "ffn_M_u", "ffn_M_phi_plus", "ffn_M_phi_minus",
                                               "ffn_log_weights", "ffn_gumbel")}
    phi = a["ffn_phi"]
    at = CH * np.arange(CH + 1)[:, None] + np.arange(DELTA)[None, :] - (CH - 1)
    padded = np.zeros((N + 2 * CH, FILTERS), phi.dtype)
    padded[CH:CH + N] = phi
    return dict(
        l3_w_t=a["attn_W"].T, l3_b_qk=a["attn_b"][:2 * C].reshape(2, C).T, l3_b_v=a["attn_b"][2 * C:].reshape(1, C),
        l3_sigma=a["ffn_sigma"], l3_phi=padded[at + CH].transpose(0, 2, 1).reshape(CH + 1, FILTERS * DELTA),
        l3_m_u=a["ffn_M_u"], l3_m_plus=a["ffn_M_phi_plus"], l3_m_minus=a["ffn_M_phi_minus"],
        l3_log_weights=a["ffn_log_weights"], l3_gumbel=a["ffn_gumbel"])


def layer3(nc, x, out, A):
    resid = nc.dram_tensor("l3_resid", (BATCH, N, C), F32).ap()
    rev = nc.dram_tensor("l3_rev", (BATCH, N, C), F32).ap()
    phi_hat = nc.dram_tensor("l3_phi_hat", (2, FREQ, FILTERS, 2, DELTA), F32).ap()
    x_hat = nc.dram_tensor("l3_x_hat", (BATCH, 2, FREQ, CH, C), F32).ap()
    y_hat = nc.dram_tensor("l3_y_hat", (BATCH, 2, FREQ, CH, C), F32).ap()
    with ExitStack() as ctx:
        st = Stage(nc, ctx, "l3")
        mats = st.sb("mats", [P, 2, FILTERS, C])
        mats_u = st.sb("mats_u", [P, LAGS, C])
        tile_mask = st.sb("tile_mask", [P, NT])
        chunk_mask = st.sb("chunk_mask", [CH, 1])
        choose_candidate(nc, A["l3_log_weights"], A["l3_gumbel"], A["l3_sigma"], A["l3_m_plus"], A["l3_m_minus"], A["l3_m_u"],
                         A["tile_in"], A["chunk_in"], mats, mats_u, tile_mask, chunk_mask)
        causal_attention_layer(nc, x, A["l3_w_t"], A["l3_b_qk"], A["l3_b_v"], A["causal"], A["ident"], A["reverse"], tile_mask,
                               mats_u, resid, rev)
        spectral_transforms(nc, rev, A["l3_phi"], A["dft_phi"], A["dft_x"], phi_hat, x_hat.rearrange("b a w s d -> b (a w) (s d)"))
        spectral_products(nc, x_hat, phi_hat, mats, A["ident"], y_hat)
        spectral_return(nc, y_hat, A["dft_y"], chunk_mask, resid, out)


def build(nc, A, out):
    x1, x2, x3 = (nc.dram_tensor(f"x{i}", (BATCH, N, C), F32).ap() for i in (1, 2, 3))
    layer0(nc, A["x"], x1, A)
    layer1(nc, x1, x2, A)
    layer2(nc, x2, x3, A)
    layer3(nc, x3, out, A)


def kernel(**inputs):
    import concourse.bacc as bacc
    from concourse.bass_utils import run_bass_kernel_spmd

    arrays = dict(x=np.asarray(inputs["x"]).reshape(BATCH, N, C), **l0_arrays(inputs), **l1_arrays(inputs), **l2_arrays(inputs),
                  **l3_arrays(inputs), **host_constants())
    arrays = {n: np.ascontiguousarray(a) for n, a in arrays.items()}
    nc = bacc.Bacc("TRN2", target_bir_lowering=False, num_devices=1)
    A = {n: nc.dram_tensor(n, a.shape, mybir.dt.from_np(a.dtype), kind="ExternalInput").ap() for n, a in arrays.items()}
    out = nc.dram_tensor("out", (BATCH, N, C), F32, kind="ExternalOutput").ap()
    build(nc, A, out)
    r = run_bass_kernel_spmd(nc, [arrays], core_ids=[0])
    return r.results[0]["out"].reshape(BATCH, H, W, C)
```
